# Optimizing a Trainium2 kernel written in Bass

```python
import numpy as np
import jax
import jax.numpy as jnp

def _softmax(x, axis=-1):
    return jax.nn.softmax(x, axis=axis)

def _gelu(x):
    return jax.nn.gelu(x, approximate=True)

def _silu(x):
    return jax.nn.silu(x)

def _sigmoid(x):
    return jax.nn.sigmoid(x)

def _layernorm(x, axis=-1, eps=1e-05):
    m = jnp.mean(x, axis=axis, keepdims=True)
    v = jnp.var(x, axis=axis, keepdims=True)
    return (x - m) / jnp.sqrt(v + eps)

def _scatter_add(tgt, idx, src, axis=0):
    return tgt.at[idx].add(src)

def _segment_sum(src, seg, n):
    return jax.ops.segment_sum(src, seg, n)
kernel_name = 'mk_macaron_d1_jaxref_r8_8a8c38'

def setup_inputs(seed: int=0):
    np.random.seed(seed)
    _w = jnp.asarray

    def _L0_attn_setup():
        import jax, jax.numpy as jnp
        import numpy as np
        import math
        D_MODEL = 512
        N_HEADS = 32
        HEAD_DIM = D_MODEL // N_HEADS
        CLIP_QKV = 8.0
        ALIBI_BIAS_MAX = 8
        LN_EPS = 1e-05

        def _alibi_slopes(total_num_heads: int, alibi_bias_max: int) -> jnp.ndarray:
            next_p2 = 2 ** math.ceil(math.log2(total_num_heads))
            m = jnp.arange(1, next_p2 + 1, dtype=jnp.float32) * (alibi_bias_max / next_p2)
            slopes = 1.0 / jnp.power(2.0, m)
            if next_p2 != total_num_heads:
                slopes = jnp.concatenate([slopes[1::2], slopes[::2]])[:total_num_heads]
            return slopes

        def _layer_norm(x, w, b):
            mu = jnp.mean(x, axis=-1, keepdims=True)
            var = jnp.var(x, axis=-1, keepdims=True)
            return (x - mu) * jax.lax.rsqrt(var + LN_EPS) * w + b
        key = jax.random.key(seed)
        k0, k1, k2 = jax.random.split(key, 3)
        B, S = (2, 256)
        return {'hidden_states': jax.random.normal(k0, (B, S, D_MODEL), dtype=jnp.float32), 'w_qkv': jax.random.normal(k1, (3 * D_MODEL, D_MODEL), dtype=jnp.float32) * 0.02, 'q_ln_w': jnp.ones((D_MODEL,), jnp.float32), 'q_ln_b': jnp.zeros((D_MODEL,), jnp.float32), 'k_ln_w': jnp.ones((D_MODEL,), jnp.float32), 'k_ln_b': jnp.zeros((D_MODEL,), jnp.float32), 'w_out': jax.random.normal(k2, (D_MODEL, D_MODEL), dtype=jnp.float32) * 0.02}
    _L0_attn_in = _L0_attn_setup()

    def _L0_ffn_setup():
        import jax, jax.numpy as jnp
        import numpy as np
        D_MODEL = 512
        D_FF = 1376
        key = jax.random.key(seed)
        k1, k2, k3, k4 = jax.random.split(key, 4)
        x = jax.random.normal(k1, (2, 256, D_MODEL), dtype=jnp.float32)
        W_gate = jax.random.normal(k2, (D_FF, D_MODEL), dtype=jnp.float32) * D_MODEL ** (-0.5)
        W_up = jax.random.normal(k3, (D_FF, D_MODEL), dtype=jnp.float32) * D_MODEL ** (-0.5)
        W_down = jax.random.normal(k4, (D_MODEL, D_FF), dtype=jnp.float32) * D_FF ** (-0.5)
        return {'x': x, 'W_gate': W_gate, 'W_up': W_up, 'W_down': W_down}
    _L0_ffn_in = _L0_ffn_setup()
    _d = {'L0_attn_hidden_states': _L0_attn_in['hidden_states'], 'L0_attn_w_qkv': _L0_attn_in['w_qkv'], 'L0_attn_q_ln_w': _L0_attn_in['q_ln_w'], 'L0_attn_q_ln_b': _L0_attn_in['q_ln_b'], 'L0_attn_k_ln_w': _L0_attn_in['k_ln_w'], 'L0_attn_k_ln_b': _L0_attn_in['k_ln_b'], 'L0_attn_w_out': _L0_attn_in['w_out'], 'L0_ffn_W_gate': _L0_ffn_in['W_gate'], 'L0_ffn_W_up': _L0_ffn_in['W_up'], 'L0_ffn_W_down': _L0_ffn_in['W_down']}
    _x0 = _d['L0_attn_hidden_states']
    _d['L0_attn_hidden_states'] = jax.random.normal(jax.random.fold_in(jax.random.key(seed), 1), (1, 1024, 512), dtype=_x0.dtype)
    del _x0
    return _d

def reference(L0_attn_hidden_states, L0_attn_w_qkv, L0_attn_q_ln_w, L0_attn_q_ln_b, L0_attn_k_ln_w, L0_attn_k_ln_b, L0_attn_w_out, L0_ffn_W_gate, L0_ffn_W_up, L0_ffn_W_down):

    def _L0_attn_ref(hidden_states, w_qkv, q_ln_w, q_ln_b, k_ln_w, k_ln_b, w_out):
        import jax, jax.numpy as jnp
        import numpy as np
        import math
        D_MODEL = 512
        N_HEADS = 32
        HEAD_DIM = D_MODEL // N_HEADS
        CLIP_QKV = 8.0
        ALIBI_BIAS_MAX = 8
        LN_EPS = 1e-05

        def _alibi_slopes(total_num_heads: int, alibi_bias_max: int) -> jnp.ndarray:
            next_p2 = 2 ** math.ceil(math.log2(total_num_heads))
            m = jnp.arange(1, next_p2 + 1, dtype=jnp.float32) * (alibi_bias_max / next_p2)
            slopes = 1.0 / jnp.power(2.0, m)
            if next_p2 != total_num_heads:
                slopes = jnp.concatenate([slopes[1::2], slopes[::2]])[:total_num_heads]
            return slopes

        def _layer_norm(x, w, b):
            mu = jnp.mean(x, axis=-1, keepdims=True)
            var = jnp.var(x, axis=-1, keepdims=True)
            return (x - mu) * jax.lax.rsqrt(var + LN_EPS) * w + b
        B, S, D = hidden_states.shape
        qkv = jnp.einsum('bsd,ed->bse', hidden_states, w_qkv)
        qkv = jnp.clip(qkv, -CLIP_QKV, CLIP_QKV)
        q, k, v = jnp.split(qkv, 3, axis=-1)
        q = _layer_norm(q, q_ln_w, q_ln_b)
        k = _layer_norm(k, k_ln_w, k_ln_b)
        q = q.reshape(B, S, N_HEADS, HEAD_DIM)
        k = k.reshape(B, S, N_HEADS, HEAD_DIM)
        v = v.reshape(B, S, N_HEADS, HEAD_DIM)
        scale = HEAD_DIM ** (-0.5)
        scores = jnp.einsum('bqhd,bkhd->bhqk', q, k) * scale
        pos = jnp.arange(S)
        rel = pos[None, :] - pos[:, None]
        slopes = _alibi_slopes(N_HEADS, ALIBI_BIAS_MAX)
        bias = slopes[:, None, None] * rel.astype(jnp.float32)
        causal = rel <= 0
        scores = jnp.where(causal[None, None], scores + bias[None], -jnp.inf)
        probs = jax.nn.softmax(scores, axis=-1)
        attn = jnp.einsum('bhqk,bkhd->bqhd', probs, v).reshape(B, S, D)
        return jnp.einsum('bsd,ed->bse', attn, w_out)

    def _L0_ffn_ref(x, W_gate, W_up, W_down):
        import jax, jax.numpy as jnp
        import numpy as np
        D_MODEL = 512
        D_FF = 1376
        out_shape = x.shape[:-1] + (W_down.shape[0],)
        xf = x.reshape(-1, x.shape[-1])
        up = jnp.einsum('td,fd->tf', xf, W_up)
        gate = jax.nn.silu(jnp.einsum('td,fd->tf', xf, W_gate))
        h = gate * up
        y = jnp.einsum('tf,df->td', h, W_down)
        return y.reshape(out_shape)
    x = L0_attn_hidden_states
    x = x + 0.5 * _L0_ffn_ref(_layernorm(x, axis=-1), L0_ffn_W_gate, L0_ffn_W_up, L0_ffn_W_down)
    x = x + _L0_attn_ref(_layernorm(x, axis=-1), L0_attn_w_qkv, L0_attn_q_ln_w, L0_attn_q_ln_b, L0_attn_k_ln_w, L0_attn_k_ln_b, L0_attn_w_out)
    x = x + 0.5 * _L0_ffn_ref(_layernorm(x, axis=-1), L0_ffn_W_gate, L0_ffn_W_up, L0_ffn_W_down)
    return x

_drawn_inputs = setup_inputs


def setup_inputs(seed=0):
    import zlib

    import numpy as np

    out = dict(_drawn_inputs(seed))
    spreads = {'L0_attn_q_ln_w': (1.0, 0.6),
     'L0_attn_q_ln_b': (0.0, 0.8),
     'L0_attn_k_ln_w': (1.0, 0.6),
     'L0_attn_k_ln_b': (0.0, 0.8)}
    factors = {}
    for name, (base, spread) in spreads.items():
        noise = np.random.default_rng([zlib.crc32(name.encode()), seed]).standard_normal(out[name].shape)
        drawn = base * np.exp(spread * noise) if base else spread * noise
        out[name] = jnp.asarray(drawn.astype(out[name].dtype))
    for name, factor in factors.items():
        out[name] = (out[name] * factor).astype(out[name].dtype)
    return out
```

```python
from contextlib import ExitStack

import numpy as np

import concourse.bass as bass
from concourse import mybir

F32 = mybir.dt.float32
F32R = mybir.dt.float32r
BF16 = mybir.dt.bfloat16
ALU = mybir.AluOpType
ACT = mybir.ActivationFunctionType
AX_X = mybir.AxisListType.X

P = 128
S = 1024
D = 512
F = 1376
H = 32
HD = D // H
NT = S // P
DT = D // P
HALF = S // 2
HT = NT // 2
FT = -(-F // P)
QH = 4
NQ = H // QH
PARTS = 3
CLIP = 8.0
EPS = 1e-5
SCALE = HD ** -0.5
MASKED = -1e30

Q_PART = (0, 1, 2, 0, 1, 0)
K_PART = (0, 0, 0, 1, 1, 2)
ROW_BIAS = len(Q_PART) * HD
N_BIAS = 4 * PARTS
ROW_MAX = ROW_BIAS + N_BIAS
N_ROWS = ROW_MAX + PARTS
VC = HD + 1
VW = 32
SLOTS = 3
RING = 3

FFN_RAW = 3 * D

RAW_FFN = (0, 2 * FT + 6)
RAW_QKV = 2 * FT
RAW_OUT = RAW_QKV + DT

MAX_CHUNKS = []
for _t in range(NT):
    for _j in range(_t // HT + 1):
        _diag = _t // HT == _j
        MAX_CHUNKS.append((_t, _j, (_t % HT + 1) * P if _diag else HALF, (_t % HT) * P if _diag else None))
KEY_GROUPS = [(b, kt, max(b * HALF, kt * P), kt // HT == b) for b in range(2) for kt in range((b + 1) * HT)]
NC = len(MAX_CHUNKS)
NG = len(KEY_GROUPS)
HALF_END = (HT - 1, NG - 1)


def steps_of(s):
    uses, chunks = [[] for _ in range(NG)], [(h, c) for h in range(QH) for c in range(NC)]
    for u in range(NG):
        if u == 2 and s > 0:
            uses[u].append(("out", 1))
        if s < NQ - 1:
            uses[u] += [("max", hc) for hc in chunks[5 * u:5 * u + 5]]
        if u == 7 and s >= 0:
            uses[u].append(("out", 0))
        if u == 10 and s < NQ - 1:
            uses[u].append(("maxT", None))
    return uses


def n_uses(s):
    return sum(map(len, steps_of(s)))


def use_base(s):
    first = n_uses(-1)
    if isinstance(s, int) and s < 0:
        return 0
    if isinstance(s, int) and s == 0:
        return first
    return (s - 1) * n_uses(1) + (first + n_uses(0))


def macaron_block(nc, x_in, w_ffn, w_qkv, w_out, ln_w, ln_b, ident_in, ident_b_in, mask_in, bias_q, bias_k, out):
    ctx = ExitStack()
    with ctx:
        at = [-(-nc.sbuf_base // 64) * 64]

        def place(name, shape, dt, offset=None):
            size = int(np.prod(shape[1:])) * (2 if dt == BF16 else 4)
            if offset is None:
                offset, at[0] = at[0], -(-(at[0] + size) // 64) * 64
            return nc.alloc_sbuf_tensor_at(name, shape, dt, offset=offset)

        def region(size):
            start, at[0] = at[0], at[0] + size
            return start

        def sem(name):
            return ctx.enter_context(nc.semaphore(name))

        KB = 1024
        x_tok = place("x_tok", [P, NT, D], F32)
        xnT_at = region(32 * KB)
        xnT_hi = place("xnT_hi", [P, DT, S], F32R, xnT_at)
        xnT_lo = place("xnT_lo", [P, DT, S], F32R, xnT_at + 16 * KB)
        raw = place("raw", [P, 2, FFN_RAW], F32)
        xn = place("xn", [P, HT, D], F32)
        v_aug = place("v_aug", [P, NT, H * VC + HD], F32)
        ident = place("ident", [P, P], F32)
        ident_b = place("ident_b", [P, P], BF16)
        masks = place("masks", [P, 2, P], BF16)
        lnw = place("lnw", [P, 2, DT], F32)
        lnb = place("lnb", [P, 2, DT], F32)
        ln_stat = place("ln_stat", [P, 2, HT, 6], F32)
        ln_mv = place("ln_mv", [P, 2, HT, 2], F32)
        ln_var = place("ln_var", [P, 2, HT], F32)
        ln_rstd = place("ln_rstd", [P, 2, HT], F32)
        minus_half = place("minus_half", [P, HT], F32)
        qk_stat = place("qk_stat", [P, 2, 2, 6], F32)
        qk_mv = place("qk_mv", [P, 2, 2, 2], F32)
        qk_var = place("qk_var", [P, 2, 2], F32)
        qk_rstd = place("qk_rstd", [P, 2, 2], F32)
        A = region(40 * KB)
        gu_hi = place("gu_hi", [P, 2, 2, DT, P], F32R, A)
        gu_lo = place("gu_lo", [P, 2, 2, DT, P], F32R, A + 8 * KB)
        dn_hi = place("dn_hi", [P, 2, D], F32R, A + 16 * KB)
        dn_lo = place("dn_lo", [P, 2, D], F32R, A + 20 * KB)
        silu = place("silu", [P, 2, HALF], F32, A + 24 * KB)
        hid = place("hid", [P, 2, HALF], F32, A + 28 * KB)
        hid_hi = place("hid_hi", [P, 2, HALF], F32R, A + 32 * KB)
        hid_lo = place("hid_lo", [P, 2, HALF], F32R, A + 36 * KB)
        parts = place("parts", [P, 2, 2, PARTS, DT, 2 * P], BF16, A)
        attn = place("attn", [P, NT, D], F32, A)
        oT = place("oT", [P, 2, HALF], F32, A + 16 * KB)
        maxp = place("maxp", [P, QH, NC], F32, A + 20 * KB)
        maxv = place("maxv", [P, QH, NT], F32, A + 20 * KB + 512)
        maxr = place("maxr", [P, QH * NT], F32, A + 21 * KB)
        max_parts = place("max_parts", [P, PARTS, QH * NT], BF16, A + 21 * KB + 512)
        maxT = place("maxT", [PARTS * QH * NT, P], BF16, A + 22 * KB)
        rsum = place("rsum", [P, 2, HT, QH], F32, A + 23 * KB)
        wout_hi = place("wout_hi", [P, DT, D], F32R, A + 24 * KB)
        wout_lo = place("wout_lo", [P, DT, D], F32R, A + 32 * KB)
        B = region(72 * KB)
        wqkv_hi = place("wqkv_hi", [P, DT, 3 * D], F32R, B)
        wqkv_lo = place("wqkv_lo", [P, DT, 3 * D], F32R, B + 24 * KB)
        qk = place("qk", [P, 2, 2, D], F32, B + 48 * KB)
        qkT = place("qkT", [P, 2, 2, DT, P], F32, B + 56 * KB)
        qkT_rest = place("qkT_rest", [P, 2, 2, DT, P], F32, B + 64 * KB)
        q_rows = place("q_rows", [P, SLOTS, QH, S], BF16, B)
        k_rows = place("k_rows", [P, SLOTS, QH, S], BF16, B + 24 * KB)
        probs = place("probs", [P, 3, QH, HALF], F32, B + 48 * KB)
        v_quad = place("v_quad", [P, SLOTS, NT, QH * VC + HD], F32, xnT_at)
        aT_hi = place("aT_hi", [P, 2, DT, P], F32R, B)
        aT_lo = place("aT_lo", [P, 2, DT, P], F32R, B + 4 * KB)

        bank = [ctx.enter_context(nc.psum_tensor(f"bank{i}", [P, 512], F32)) for i in range(8)]
        gate_ps, up_ps, y_ps = bank[0:2], bank[2:4], bank[4:8]
        lnT_ps = bank[0:4]
        qkv_ps, qkT_ps = [bank[0:3], bank[3:6]], bank[6:8]
        ring_a, ring_b, o_ps = bank[0:3], bank[3:6], bank[6:8]
        proj_ps, attnT_ps = bank[4:6], bank[6:8]

        qk_scr = nc.dram_tensor("qk_scr", (2, PARTS, D, S), BF16, kind="Internal").ap()
        max_scr = nc.dram_tensor("max_scr", (2, PARTS, QH * S), BF16, kind="Internal").ap()

        const_in = sem("const_in")
        x_loaded = [sem(f"x_loaded{i}") for i in range(NT)]
        raw_in = [sem(f"raw_in{i}") for i in range(2)]
        w_hi = sem("w_hi")
        w_lo = sem("w_lo")
        half_set = sem("half_set")
        q_scaled = sem("q_scaled")
        v_ones = sem("v_ones")
        ln_stats = sem("ln_stats")
        ln_mean = sem("ln_mean")
        ln_eps = sem("ln_eps")
        ln_rs = sem("ln_rs")
        ln_normed = sem("ln_normed")
        ln_turned = sem("ln_turned")
        ln_hi = sem("ln_hi")
        ln_lo = sem("ln_lo")
        gate_done = sem("gate_done")
        up_done = sem("up_done")
        down_done = sem("down_done")
        y_done = sem("y_done")
        silu_done = sem("silu_done")
        hid_done = sem("hid_done")
        hid_hi_done = sem("hid_hi_done")
        hid_lo_done = sem("hid_lo_done")
        x_added = sem("x_added")
        qkv_done = sem("qkv_done")
        clipped = sem("clipped")
        qk_stats = sem("qk_stats")
        qk_mean = sem("qk_mean")
        qk_eps = sem("qk_eps")
        qk_rs = sem("qk_rs")
        qk_normed = sem("qk_normed")
        qk_turned = sem("qk_turned")
        qkT_done = sem("qkT_done")
        part0_done = sem("part0_done")
        rest1_done = sem("rest1_done")
        part1_done = sem("part1_done")
        part2_done = sem("part2_done")
        parts_out = [sem(f"parts_out{i}") for i in range(2)]
        rows_in = [sem(f"rows_in{i}") for i in range(SLOTS)]
        max_out = sem("max_out")
        max_in = [sem(f"max_in{i}") for i in range(SLOTS)]
        ring_a_done = sem("ring_a_done")
        ring_a_used = sem("ring_a_used")
        ring_b_done = sem("ring_b_done")
        probs_done = sem("probs_done")
        pv_done = sem("pv_done")
        oT_done = sem("oT_done")
        max_step = sem("max_step")
        max_parts_done = sem("max_parts_done")
        rsum_done = sem("rsum_done")
        attn_turned = sem("attn_turned")
        aT_hi_done = sem("aT_hi_done")
        aT_lo_done = sem("aT_lo_done")
        proj_done = sem("proj_done")
        out_sent = sem("out_sent")

        def atleast(eng, s, value):
            if not isinstance(value, int) or value > 0:
                eng.wait_ge(s, value)

        def wait_down(eng, half, k):
            if not isinstance(k, int) or k >= 2:
                eng.wait_ge(down_done, k + ((FT - 1) * half - 1))
            elif half and k == 0:
                eng.wait_ge(down_done, (FT - 1) * half)
            elif half:
                eng.wait_ge(y_done, HT * half)

        def wait_raw_at(eng, r):
            eng.wait_ge(raw_in[r % 2], 16 * (r // 2 + 1))

        def wait_raw(eng, r0, k, parity):
            eng.wait_ge(raw_in[(r0 + parity) % 2], (k + (r0 - (r0 + parity) % 2 + 2)) * 8)

        last_use = use_base(NQ - 1) + n_uses(NQ - 1) + 1


        def out_use(s, b):
            at_step = s + b
            if isinstance(at_step, int) and at_step == NQ:
                return last_use
            kind = at_step if isinstance(at_step, int) else 1
            k = 0
            for group in steps_of(kind):
                for use in group:
                    k += 1
                    if use == ("out", b):
                        return use_base(at_step) + k
            raise ValueError(b)

        def last_out(pe):
            k = last_use - 1
            pe.wait_ge(ring_a_used, k + 1 - RING)
            pe.wait_ge(oT_done, 2 * NQ)
            for t in range(HT):
                ins = pe.transpose(ring_a[k % RING][:, t * P:(t + 1) * P], oT[:, 1, t * P:(t + 1) * P], ident[:, :])
            ins.then_inc(ring_a_done, 1)

        constants = ((ident, ident_in), (ident_b, ident_b_in), (masks, mask_in), (lnw, ln_w), (lnb, ln_b))
        block = ctx.enter_context(nc.Block())

        @block.sync
        def _(sp):
            for t in range(NT):
                sp.dma_start(x_tok[:, t, :], x_in[t * P:(t + 1) * P, :]).then_inc(x_loaded[t], 16)
                if t == 0:
                    for dst, src in constants:
                        sp.dma_start(dst[tuple(slice(None) for _ in src.shape)], src).then_inc(const_in, 16)

            def load_raw(r, parity, src, width):
                atleast(sp, w_hi, 2 * r - 2)
                atleast(sp, w_lo, 2 * r - 2)
                sp.dma_start(raw[:, parity, 0:width], src).then_inc(raw_in[parity], 16)

            def load_ffn(n):
                for b in range(2):
                    r0 = RAW_FFN[n] + b * FT
                    load_raw(r0, r0 % 2, w_ffn[0], FFN_RAW)
                    with sp.Fori(0, (FT - 1) // 2) as i:
                        for c in range(2):
                            load_raw(i * 2 + (r0 + 1 + c), (r0 + 1 + c) % 2, w_ffn[i * 2 + (1 + c)], FFN_RAW)

            load_ffn(0)
            for dt in range(DT):
                load_raw(RAW_QKV + dt, (RAW_QKV + dt) % 2, w_qkv[dt], 3 * D)
            for j in range(2):
                load_raw(RAW_OUT + j, (RAW_OUT + j) % 2, w_out[j], 2 * D)

            for j in range(NT // 2):
                sp.wait_ge(part2_done, 2 * j + 2)
                for c in range(2):
                    for part in range(PARTS):
                        dst = qk_scr[c, part].rearrange("(n r) t -> r n t", r=P)[:, :, j * 2 * P:(j + 1) * 2 * P]
                        sp.dma_start(dst, parts[:, j % 2, c, part, :, :]).then_inc(parts_out[j % 2], 16)
            for j in range(2):
                sp.wait_ge(parts_out[j], 16 * 2 * PARTS * NT // 4)
            sp.wait_ge(clipped, 3 * NT)

            def load_quad(g):
                slot = g % SLOTS
                for grp in range(len(Q_PART)):
                    for c, which, rows in ((0, Q_PART, q_rows), (1, K_PART, k_rows)):
                        src = qk_scr[c, which[grp], g * QH * HD:(g + 1) * QH * HD, :]
                        sp.dma_start(rows[grp * HD:(grp + 1) * HD, slot, :, :],
                                     src.rearrange("(h d) t -> d h t", d=HD)).then_inc(rows_in[slot], 16)
                sp.dma_start(q_rows[ROW_BIAS:ROW_MAX, slot, :, :], bias_q[g]).then_inc(rows_in[slot], 16)
                sp.dma_start(k_rows[ROW_BIAS:N_ROWS, slot, :, :], bias_k[g]).then_inc(rows_in[slot], 16)
                sp.dma_start(v_quad[:, slot, :, :],
                             v_aug[:, :, g * QH * VC:(g + 1) * QH * VC + HD]).then_inc(rows_in[slot], 16)

            def move_max(g):
                sp.wait_ge(ring_a_used, use_base(g - 1) + n_uses(g - 1))
                if g >= 2:
                    sp.wait_ge(max_in[(g - 2) % SLOTS], 16 * ((g - 2) // SLOTS + 1))
                sp.dma_start(max_scr[g % 2].rearrange("p (r c) -> (p r) c", c=P), maxT[:, :]).then_inc(max_out, 16)
                sp.wait_ge(max_out, 16 * (g + 1))
                sp.dma_start(q_rows[ROW_MAX:N_ROWS, g % SLOTS, :, :],
                             max_scr[g % 2].rearrange("p (h t) -> p h t", h=QH)).then_inc(max_in[g % SLOTS], 16)

            for g in range(SLOTS):
                load_quad(g)
            move_max(0)
            for s in range(NQ - 1):
                move_max(s + 1)
                if s + SLOTS < NQ:
                    sp.wait_ge(pv_done, NG * (s + 1))
                    load_quad(s + SLOTS)

            load_ffn(1)
            for t in range(NT):
                sp.wait_ge(x_added, 2 * NT + t + 1)
                sp.dma_start(out[t * P:(t + 1) * P, :], x_tok[:, t, :]).then_inc(out_sent, 16)
            sp.wait_ge(out_sent, 16 * NT)

        @block.gpsimd
        def _(pool):
            pool.memset(minus_half[:, :], -0.5).then_inc(half_set, 1)
            pool.wait_ge(half_set, 1)

            def rsqrt(mv_ready, count, mv, var, rstd, eps_sem, rs_sem, done):
                pool.wait_ge(mv_ready, count)
                pool.tensor_scalar(var, mv, EPS, None, ALU.add).then_inc(eps_sem, 1)
                pool.wait_ge(eps_sem, done)
                pool.tensor_tensor(rstd, var, minus_half[:, 0:var.shape[1]], ALU.pow).then_inc(rs_sem, 1)

            def ln(l):
                b = l % 2
                rsqrt(ln_mean, HT * (l + 1), ln_mv[:, b, :, 1], ln_var[:, b, :], ln_rstd[:, b, :],
                      ln_eps, ln_rs, l + 1)

            pool.wait_ge(const_in, 16 * len(constants))
            for a in (lnw, lnb):
                pool.tensor_scalar(a[:, 0, :], a[:, 0, :], SCALE, None, ALU.mult).then_inc(q_scaled, 1)
            for l in range(2):
                ln(l)
            pool.memset(v_aug[:, :, :], 1.0).then_inc(v_ones, 1)
            for l in range(2, 4):
                ln(l)
            def rest2(t):
                pool.wait_ge(part1_done, t + 1)
                for c in range(2):
                    ins = pool.tensor_tensor(
                        parts[:, (t // 2) % 2, c, 2, :, (t % 2) * P:(t % 2 + 1) * P], qkT_rest[:, t % 2, c, :, :],
                        parts[:, (t // 2) % 2, c, 1, :, (t % 2) * P:(t % 2 + 1) * P], ALU.subtract)
                ins.then_inc(part2_done, 1)

            for t in range(NT):
                rsqrt(qk_mean, t + 1, qk_mv[:, t % 2, :, 1], qk_var[:, t % 2, :], qk_rstd[:, t % 2, :],
                      qk_eps, qk_rs, t + 1)
                if t > 0:
                    rest2(t - 1)
            rest2(NT - 1)
            for l in range(4, 6):
                ln(l)

        @block.tensor
        def _(pe):
            def three_pass(dst, a_hi, a_lo, b_hi, b_lo, start, stop):
                pe.matmul(dst, a_hi, b_hi, start=start, stop=False)
                pe.matmul(dst, a_hi, b_lo, start=False, stop=False)
                return pe.matmul(dst, a_lo, b_hi, start=False, stop=stop)

            def ln_turn(l):
                for t in range(HT):
                    n = HT * l + t
                    pe.wait_ge(ln_normed, n + 1)
                    atleast(pe, ln_lo, n + 1 - HT)
                    for dt in range(DT):
                        ins = pe.transpose(lnT_ps[t][:, dt * P:(dt + 1) * P], xn[:, t, dt * P:(dt + 1) * P],
                                           ident[:, :])
                    ins.then_inc(ln_turned, 1)

            def ffn(n, b):
                r0, k0, y0 = RAW_FFN[n] + b * FT, (2 * n + b) * FT, 2 * n + b
                tok = slice(b * HALF, (b + 1) * HALF)

                def gate_up(k, parity):
                    slot = (k0 + parity) % 2
                    pe.wait_ge(w_hi, k * 2 + (2 * r0 + 1))
                    pe.wait_ge(w_lo, k * 2 + (2 * r0 + 1))
                    for which, ps, freed, done in ((0, gate_ps, silu_done, gate_done), (1, up_ps, hid_done, up_done)):
                        atleast(pe, freed, k + (k0 - 1))
                        for dt in range(DT):
                            ins = three_pass(ps[slot][:, :], gu_hi[:, slot, which, dt, :], gu_lo[:, slot, which, dt, :],
                                             xnT_hi[:, dt, tok], xnT_lo[:, dt, tok], dt == 0, dt == DT - 1)
                        ins.then_inc(done, 1)

                def down(k, parity, first=False, last=False):
                    slot = (k0 + parity) % 2
                    pe.wait_ge(w_hi, k * 2 + (2 * r0 + 2))
                    pe.wait_ge(w_lo, k * 2 + (2 * r0 + 2))
                    pe.wait_ge(hid_lo_done, k + (k0 + 1))
                    for t in range(HT):
                        if first and y0:
                            pe.wait_ge(x_added, 2 * NT if y0 == 2 else (2 * NT if n else 0) + t + 1)
                        cols = slice(t * P, (t + 1) * P)
                        ins = three_pass(y_ps[t][:, :], hid_hi[:, slot, cols], hid_lo[:, slot, cols],
                                         dn_hi[:, slot, :], dn_lo[:, slot, :], first, last)
                        if last:
                            ins.then_inc(y_done, 1)
                    if not last:
                        ins.then_inc(down_done, 1)

                pe.wait_ge(ln_lo, HT * (2 * n + b + (2 if n else 0) + 1))
                gate_up(0, 0)
                gate_up(1, 1)
                down(0, 0, first=True)
                with pe.Fori(0, (FT - 3) // 2) as i:
                    gate_up(i * 2 + 2, 0)
                    down(i * 2 + 1, 1)
                    gate_up(i * 2 + 3, 1)
                    down(i * 2 + 2, 0)
                gate_up(FT - 1, 0)
                down(FT - 2, 1)
                down(FT - 1, 0, last=True)

            pe.wait_ge(const_in, 16 * len(constants))
            ln_turn(0)
            ln_turn(1)
            ffn(0, 0)
            ffn(0, 1)
            ln_turn(2)
            ln_turn(3)

            def project(t):
                if t == 0:
                    pe.wait_ge(w_hi, 2 * (RAW_QKV + DT))
                    pe.wait_ge(w_lo, 2 * (RAW_QKV + DT))
                    pe.wait_ge(ln_lo, HT * 4)
                cols = slice(t * P, (t + 1) * P)
                for c in range(3):
                    atleast(pe, clipped, 3 * (t - 2) + c + 1)
                    for dt in range(DT):
                        w = slice(c * D, (c + 1) * D)
                        ins = three_pass(qkv_ps[t % 2][c][:, :], xnT_hi[:, dt, cols], xnT_lo[:, dt, cols],
                                         wqkv_hi[:, dt, w], wqkv_lo[:, dt, w], dt == 0, dt == DT - 1)
                    ins.then_inc(qkv_done, 1)

            def qk_turn(t):
                pe.wait_ge(qk_normed, t + 1)
                atleast(pe, qkT_done, t)
                for c in range(2):
                    for dt in range(DT):
                        ins = pe.transpose(qkT_ps[c][:, dt * P:(dt + 1) * P], qk[:, t % 2, c, dt * P:(dt + 1) * P],
                                           ident[:, :])
                ins.then_inc(qk_turned, 1)

            for t in range(NT):
                project(t)
                if t > 0:
                    qk_turn(t - 1)
            qk_turn(NT - 1)

            def ring_a_use(s, k, parity, use, slot, next_slot):
                kind, what = use
                ps = ring_a[(parity + k) % RING]
                atleast(pe, ring_a_used, use_base(s) + (k + 1 - RING))
                if kind == "max":
                    h, c = what
                    t, j, width, diag = MAX_CHUNKS[c]
                    ins = pe.matmul(ps[:, 0:width], q_rows[0:ROW_MAX, next_slot, h, t * P:(t + 1) * P],
                                    k_rows[0:ROW_MAX, next_slot, h, j * HALF:j * HALF + width],
                                    start=True, stop=diag is None)
                    if diag is not None:
                        ins = pe.matmul(ps[:, diag:diag + P], ident_b[:, :], masks[:, 0, :], start=False, stop=True)
                elif kind == "out":
                    b = what
                    pe.wait_ge(oT_done, s * 2 + (1 if b == 0 else 0))
                    for t in range(HT):
                        ins = pe.transpose(ps[:, t * P:(t + 1) * P], oT[:, b, t * P:(t + 1) * P], ident[:, :])
                else:
                    pe.wait_ge(max_parts_done, s + 2)
                    ins = pe.transpose(ps[0:PARTS * QH * NT, 0:P // 2].bitcast(BF16),
                                       max_parts[:, :, :].rearrange("p a b -> p (a b)"), ident_b[:, :])
                ins.then_inc(ring_a_done, 1)

            def scores(s, u, h, slot):
                b, kt, q0, diag = KEY_GROUPS[u]
                width = (b + 1) * HALF - q0
                ps = ring_b[(QH * u + h) % RING]
                atleast(pe, probs_done, s * (NG * QH) + (QH * u + h + 1 - RING))
                args = (ps[:, 0:width], k_rows[0:N_ROWS, slot, h, kt * P:(kt + 1) * P],
                        q_rows[0:N_ROWS, slot, h, q0:q0 + width])
                ins = pe.matmul(*args, start=True, stop=not diag)
                if diag:
                    ins = pe.matmul(ps[:, 0:P], ident_b[:, :], masks[:, 1, :], start=False, stop=True)
                ins.then_inc(ring_b_done, 1)

            def values(s, u, slot):
                b, kt, q0, diag = KEY_GROUPS[u]
                pe.wait_ge(probs_done, s * (NG * QH) + QH * (u + 1))
                if kt == 0:
                    atleast(pe, oT_done, s * 2 + (b - 1))
                for h in range(QH):
                    ins = pe.matmul(o_ps[b][VW * h:VW * (h + 1), q0 - b * HALF:HALF],
                                    v_quad[:, slot, kt, h * VC:h * VC + VW], probs[:, u % 3, h, 0:(b + 1) * HALF - q0],
                                    start=kt == 0, stop=u in HALF_END)
                ins.then_inc(pv_done, 1)

            def step(s, slot, parity, kind):
                next_slot = (slot + 1) % SLOTS
                uses = steps_of(kind)
                if kind < NQ - 1:
                    rows_wait(s, next_slot, kind)
                k = 0
                for u in range(NG):
                    todo = list(uses[u])
                    for h in range(QH):
                        if todo:
                            ring_a_use(s, k, parity, todo.pop(0), slot, next_slot)
                            k += 1
                        if kind >= 0:
                            if u == 0 and h == 0:
                                max_wait(s, slot)
                            scores(s, u, h, slot)
                    for use in todo:
                        ring_a_use(s, k, parity, use, slot, next_slot)
                        k += 1
                    if kind >= 0 and u > 0:
                        values(s, u - 1, slot)
                if kind >= 0:
                    values(s, NG - 1, slot)

            n_rows_dma = 2 * len(Q_PART) + 3

            def rows_wait(s, next_slot, kind):
                if isinstance(s, int):
                    pe.wait_ge(rows_in[next_slot], 16 * n_rows_dma * ((s + 1) // SLOTS + 1))
                else:
                    pe.wait_ge(rows_in[next_slot], loop_turn[0] * (16 * n_rows_dma) + 16 * n_rows_dma * loop_turn[1])

            def max_wait(s, slot):
                if isinstance(s, int):
                    pe.wait_ge(max_in[slot], 16 * (s // SLOTS + 1))
                else:
                    pe.wait_ge(max_in[slot], loop_turn[0] * 16 + 16 * loop_turn[2])

            loop_turn = [None, 0, 0]
            parity0 = (n_uses(-1) + n_uses(0)) % RING
            assert n_uses(1) % RING == 0
            step(-1, SLOTS - 1, 0, -1)
            step(0, 0, n_uses(-1) % RING, 0)
            with pe.Fori(0, (NQ - 2) // SLOTS) as i:
                for c in range(SLOTS):
                    loop_turn[:] = [i, (2 + c) // SLOTS + 1, (1 + c) // SLOTS + 1]
                    step(i * SLOTS + (1 + c), (1 + c) % SLOTS, parity0, 1)
            step(NQ - 1, (NQ - 1) % SLOTS, parity0, NQ - 1)
            last_out(pe)

            def attn_turn(t):
                pe.wait_ge(ring_a_used, last_use)
                atleast(pe, aT_lo_done, t - 1)
                for dt in range(DT):
                    ins = pe.transpose(attnT_ps[t % 2][:, dt * P:(dt + 1) * P], attn[:, t, dt * P:(dt + 1) * P],
                                       ident[:, :])
                ins.then_inc(attn_turned, 1)

            def out_project(t):
                pe.wait_ge(aT_lo_done, t + 1)
                atleast(pe, x_added, NT + t - 1)
                for dt in range(DT):
                    ins = three_pass(proj_ps[t % 2][:, :], aT_hi[:, t % 2, dt, :], aT_lo[:, t % 2, dt, :],
                                     wout_hi[:, dt, :], wout_lo[:, dt, :], dt == 0, dt == DT - 1)
                ins.then_inc(proj_done, 1)

            pe.wait_ge(w_hi, 2 * (RAW_OUT + 2))
            pe.wait_ge(w_lo, 2 * (RAW_OUT + 2))
            attn_turn(0)
            for t in range(NT):
                if t + 1 < NT:
                    attn_turn(t + 1)
                out_project(t)
            ln_turn(4)
            ln_turn(5)
            ffn(1, 0)
            ffn(1, 1)

        @block.scalar
        def _(act):
            def ln_round(l):
                b = l % 2
                for t in range(HT):
                    n = HT * l + t
                    cols = slice((b * HT + t) * P, (b * HT + t + 1) * P)
                    act.wait_ge(ln_turned, n + 1)
                    act.activation(xnT_hi[:, :, cols], lnT_ps[t][:, :].rearrange("p (a b) -> p a b", b=P),
                                   ACT.Copy).then_inc(ln_hi, 1)

            def hi_of(dst, src):
                act.activation(dst, src, ACT.Copy).then_inc(w_hi, 1)

            def ffn(n, b):
                r0, k0 = RAW_FFN[n] + b * FT, (2 * n + b) * FT

                def round_gate_up(k, parity):
                    slot, rs = (k0 + parity) % 2, (r0 + parity) % 2
                    wait_raw(act, r0, k, parity)
                    atleast(act, up_done, k + (k0 - 1))
                    hi_of(gu_hi[:, slot, :, :, :].rearrange("p a b c -> p (a b c)"), raw[:, rs, 0:2 * D])

                def round_down(k, parity):
                    slot, rs = (k0 + parity) % 2, (r0 + parity) % 2
                    wait_down(act, 2 * n + b, k)
                    hi_of(dn_hi[:, slot, :], raw[:, rs, 2 * D:])

                def step(k, parity, more=True):
                    slot = (k0 + parity) % 2
                    if more:
                        round_gate_up(k + 1, 1 - parity)
                    act.wait_ge(gate_done, k + (k0 + 1))
                    atleast(act, hid_done, k + (k0 - 1))
                    act.activation(silu[:, slot, :], gate_ps[slot][:, :], ACT.Silu).then_inc(silu_done, 1)
                    act.wait_ge(hid_done, k + (k0 + 1))
                    wait_down(act, 2 * n + b, k)
                    act.activation(hid_hi[:, slot, :], hid[:, slot, :], ACT.Copy).then_inc(hid_hi_done, 1)
                    if more:
                        round_down(k + 1, 1 - parity)

                round_gate_up(0, 0)
                round_down(0, 0)
                for k in range(2):
                    step(k, k)
                with act.Fori(0, (FT - 3) // 2) as i:
                    step(i * 2 + 2, 0)
                    step(i * 2 + 3, 1)
                step(FT - 1, 0, more=False)

            ln_round(0)
            ln_round(1)
            ffn(0, 0)
            ffn(0, 1)
            ln_round(2)
            ln_round(3)
            for dt in range(DT):
                wait_raw_at(act, RAW_QKV + dt)
                for piece in range(2):
                    cols = slice(piece * 768, piece * 768 + 768)
                    hi_of(wqkv_hi[:, dt, cols], raw[:, (RAW_QKV + dt) % 2, cols])
            act.wait_ge(q_scaled, 2)
            for t in range(NT):
                slot, pair, cols = t % 2, (t // 2) % 2, slice((t % 2) * P, (t % 2 + 1) * P)
                act.wait_ge(qk_turned, t + 1)
                atleast(act, rest1_done, t - 1)
                for c in range(2):
                    for dt in range(DT):
                        ins = act.activation(qkT[:, slot, c, dt, :], qkT_ps[c][:, dt * P:(dt + 1) * P], ACT.Identity,
                                             bias=lnb[:, c, dt:dt + 1], scale=lnw[:, c, dt:dt + 1])
                ins.then_inc(qkT_done, 1)
                act.wait_ge(qkT_done, t + 1)
                if t % 2 == 0 and t >= 4:
                    act.wait_ge(parts_out[pair], 16 * 2 * PARTS)
                for c in range(2):
                    ins = act.activation(parts[:, pair, c, 0, :, cols], qkT[:, slot, c, :, :], ACT.Copy)
                ins.then_inc(part0_done, 1)
                act.wait_ge(rest1_done, t + 1)
                for c in range(2):
                    ins = act.activation(parts[:, pair, c, 1, :, cols], qkT_rest[:, slot, c, :, :], ACT.Copy)
                ins.then_inc(part1_done, 1)

            for j in range(2):
                wait_raw_at(act, RAW_OUT + j)
                for piece in range(2):
                    hi_of(wout_hi[:, 2 * j + piece, :], raw[:, (RAW_OUT + j) % 2, piece * D:(piece + 1) * D])

            def read_outputs(s, b):
                act.wait_ge(pv_done, s * NG + (HALF_END[b] + 1))
                if not (isinstance(s, int) and s == 0):
                    act.wait_ge(ring_a_done, out_use(s - 1, b))
                act.activation(oT[:, b, :], o_ps[b][:, :], ACT.Copy).then_inc(oT_done, 1)

            def step(s, kind):
                for u in range(NG):
                    b, kt, q0, diag = KEY_GROUPS[u]
                    width = (b + 1) * HALF - q0
                    atleast(act, pv_done, s * NG + (u - 2))
                    for h in range(QH):
                        act.wait_ge(ring_b_done, s * (NG * QH) + (QH * u + h + 1))
                        act.activation(probs[:, u % 3, h, 0:width], ring_b[(QH * u + h) % RING][:, 0:width],
                                       ACT.Exp).then_inc(probs_done, 1)
                    if u == 0 and kind > 0:
                        read_outputs(s - 1, 1)
                    if u == HALF_END[0] + 1:
                        read_outputs(s, 0)

            step(0, 0)
            with act.Fori(0, (NQ - 2) // SLOTS) as i:
                for c in range(SLOTS):
                    step(i * SLOTS + (1 + c), 1)
            step(NQ - 1, 1)
            read_outputs(NQ - 1, 1)

            for t in range(NT):
                act.wait_ge(attn_turned, t + 1)
                atleast(act, proj_done, t - 1)
                act.activation(aT_hi[:, t % 2, :, :], attnT_ps[t % 2][:, :].rearrange("p (a b) -> p a b", b=P),
                               ACT.Copy).then_inc(aT_hi_done, 1)
            ln_round(4)
            ln_round(5)
            act.wait_ge(proj_done, NT)
            ffn(1, 0)
            ffn(1, 1)

        @block.vector
        def _(dve):
            def ln_norm(l):
                b = l % 2
                for t in range(HT):
                    if l < 2:
                        dve.wait_ge(x_loaded[b * HT + t], 16)
                    else:
                        dve.wait_ge(x_added, (l // 2 - 1) * NT + b * HT + t + 1)
                    dve.bn_stats(ln_stat[:, b, t, :], x_tok[:, b * HT + t, :]).then_inc(ln_stats, 1)
                for t in range(HT):
                    dve.wait_ge(ln_stats, HT * l + t + 1)
                    dve.bn_aggr(ln_mv[:, b, t, :], ln_stat[:, b, t, :]).then_inc(ln_mean, 1)
                dve.wait_ge(ln_mean, HT * (l + 1))
                dve.wait_ge(ln_rs, l + 1)
                for t in range(HT):
                    atleast(dve, ln_turned, HT * (l - 1) + t + 1)
                    dve.tensor_scalar(xn[:, t, :], x_tok[:, b * HT + t, :], ln_mv[:, b, t, 0:1],
                                      ln_rstd[:, b, t:t + 1], ALU.subtract, ALU.mult).then_inc(ln_normed, 1)

            def ln_rest(l):
                b = l % 2
                for t in range(HT):
                    n = HT * l + t
                    cols = slice((b * HT + t) * P, (b * HT + t + 1) * P)
                    dve.wait_ge(ln_hi, n + 1)
                    dve.tensor_tensor(xnT_lo[:, :, cols], lnT_ps[t][:, :].rearrange("p (a b) -> p a b", b=P),
                                      xnT_hi[:, :, cols].bitcast(F32), ALU.subtract).then_inc(ln_lo, 1)

            def lo_of(dst, src, hi):
                dve.tensor_tensor(dst, src, hi.bitcast(F32), ALU.subtract).then_inc(w_lo, 1)

            def ffn(n, b):
                r0, k0 = RAW_FFN[n] + b * FT, (2 * n + b) * FT

                def split_gate_up(k, parity):
                    slot, rs = (k0 + parity) % 2, (r0 + parity) % 2
                    wait_raw(dve, r0, k, parity)
                    dve.wait_ge(w_hi, k * 2 + (2 * r0 + 1))
                    atleast(dve, up_done, k + (k0 - 1))
                    lo_of(gu_lo[:, slot, :, :, :].rearrange("p a b c -> p (a b c)"), raw[:, rs, 0:2 * D],
                          gu_hi[:, slot, :, :, :].rearrange("p a b c -> p (a b c)"))

                def split_down(k, parity):
                    slot, rs = (k0 + parity) % 2, (r0 + parity) % 2
                    dve.wait_ge(w_hi, k * 2 + (2 * r0 + 2))
                    wait_down(dve, 2 * n + b, k)
                    lo_of(dn_lo[:, slot, :], raw[:, rs, 2 * D:], dn_hi[:, slot, :])

                def step(k, parity, more=True):
                    slot = (k0 + parity) % 2
                    if more:
                        split_gate_up(k + 1, 1 - parity)
                    dve.wait_ge(silu_done, k + (k0 + 1))
                    dve.wait_ge(up_done, k + (k0 + 1))
                    atleast(dve, hid_lo_done, k + (k0 - 1))
                    atleast(dve, hid_hi_done, k + (k0 - 1))
                    dve.tensor_tensor(hid[:, slot, :], up_ps[slot][:, :], silu[:, slot, :],
                                      ALU.mult).then_inc(hid_done, 1)
                    dve.wait_ge(hid_hi_done, k + (k0 + 1))
                    dve.wait_ge(hid_done, k + (k0 + 1))
                    wait_down(dve, 2 * n + b, k)
                    dve.tensor_tensor(hid_lo[:, slot, :], hid[:, slot, :], hid_hi[:, slot, :].bitcast(F32),
                                      ALU.subtract).then_inc(hid_lo_done, 1)
                    if more:
                        split_down(k + 1, 1 - parity)

                split_gate_up(0, 0)
                split_down(0, 0)
                for k in range(2):
                    step(k, k)
                with dve.Fori(0, (FT - 3) // 2) as i:
                    step(i * 2 + 2, 0)
                    step(i * 2 + 3, 1)
                step(FT - 1, 0, more=False)
                for t in range(HT):
                    dve.wait_ge(y_done, HT * (2 * n + b) + t + 1)
                    dve.scalar_tensor_tensor(out=x_tok[:, b * HT + t, :], in0=y_ps[t][:, :], scalar=0.5,
                                             in1=x_tok[:, b * HT + t, :], op0=ALU.mult,
                                             op1=ALU.add).then_inc(x_added, 1)

            ln_norm(0)
            ln_norm(1)
            ln_rest(0)
            ln_rest(1)
            ffn(0, 0)
            ffn(0, 1)
            ln_norm(2)
            ln_norm(3)
            ln_rest(2)
            ln_rest(3)
            for dt in range(DT):
                wait_raw_at(dve, RAW_QKV + dt)
                for piece in range(2):
                    cols = slice(piece * 768, piece * 768 + 768)
                    dve.wait_ge(w_hi, 2 * (RAW_QKV + dt) + piece + 1)
                    lo_of(wqkv_lo[:, dt, cols], raw[:, (RAW_QKV + dt) % 2, cols], wqkv_hi[:, dt, cols])

            dve.wait_ge(v_ones, 1)

            def qk_norm(t):
                slot = t % 2
                for c in range(3):
                    dve.wait_ge(qkv_done, 3 * t + c + 1)
                    src = qkv_ps[slot][c][:, :]
                    if c < 2:
                        atleast(dve, qk_turned, t - 1)
                        dst = qk[:, slot, c, :]
                    else:
                        dst = v_aug[:, t, 0:H * VC].rearrange("p (h c) -> p h c", c=VC)[:, :, 0:HD]
                        src = src.rearrange("p (h c) -> p h c", c=HD)
                    dve.tensor_scalar(dst, src, CLIP, -CLIP, ALU.min, ALU.max).then_inc(clipped, 1)
                for c in range(2):
                    dve.wait_ge(clipped, 3 * t + c + 1)
                    dve.bn_stats(qk_stat[:, slot, c, :], qk[:, slot, c, :]).then_inc(qk_stats, 1)
                for c in range(2):
                    dve.wait_ge(qk_stats, 2 * t + c + 1)
                    ins = dve.bn_aggr(qk_mv[:, slot, c, :], qk_stat[:, slot, c, :])
                ins.then_inc(qk_mean, 1)
                dve.wait_ge(qk_mean, t + 1)
                dve.wait_ge(qk_rs, t + 1)
                for c in range(2):
                    ins = dve.tensor_scalar(qk[:, slot, c, :], qk[:, slot, c, :], qk_mv[:, slot, c, 0:1],
                                            qk_rstd[:, slot, c:c + 1], ALU.subtract, ALU.mult)
                ins.then_inc(qk_normed, 1)

            def rest1(t):
                slot, pair, cols = t % 2, (t // 2) % 2, slice((t % 2) * P, (t % 2 + 1) * P)
                dve.wait_ge(part0_done, t + 1)
                atleast(dve, part2_done, t - 1)
                for c in range(2):
                    ins = dve.tensor_tensor(qkT_rest[:, slot, c, :, :], qkT[:, slot, c, :, :],
                                            parts[:, pair, c, 0, :, cols], ALU.subtract)
                ins.then_inc(rest1_done, 1)

            for t in range(NT):
                qk_norm(t)
                if t > 0:
                    rest1(t - 1)
            rest1(NT - 1)
            for j in range(2):
                wait_raw_at(dve, RAW_OUT + j)
                for piece in range(2):
                    dve.wait_ge(w_hi, 2 * (RAW_OUT + j) + piece + 1)
                    lo_of(wout_lo[:, 2 * j + piece, :], raw[:, (RAW_OUT + j) % 2, piece * D:(piece + 1) * D],
                          wout_hi[:, 2 * j + piece, :])

            def ring_a_use(s, k, parity, use):
                kind, what = use
                ps = ring_a[(parity + k) % RING]
                if kind == "maxT":
                    split_max(s)
                dve.wait_ge(ring_a_done, use_base(s) + (k + 1))
                if kind == "max":
                    h, c = what
                    dve.reduce_max(maxp[:, h, c:c + 1], ps[:, 0:MAX_CHUNKS[c][2]], AX_X).then_inc(ring_a_used, 1)
                elif kind == "maxT":
                    if not (isinstance(s, int) and s < 0):
                        dve.wait_ge(max_out, s * 16 + 16)
                    dve.tensor_copy(maxT[:, :], ps[0:PARTS * QH * NT, 0:P // 2].bitcast(BF16)).then_inc(ring_a_used, 1)
                else:
                    store_outputs(s - what, what, ps)

            def split_max(s):
                n0 = (s + 1) * 5
                dve.wait_ge(ring_a_used, use_base(s) + (n_uses(s if isinstance(s, int) else 1) - 1))
                dve.tensor_tensor(maxv[:, :, HT:NT], maxp[:, :, HT:NC:2], maxp[:, :, HT + 1:NC:2],
                                  ALU.max).then_inc(max_step, 1)
                dve.tensor_copy(maxv[:, :, 0:HT], maxp[:, :, 0:HT]).then_inc(max_step, 1)
                dve.wait_ge(max_step, n0 + 2)
                flat = maxv[:, :, :].rearrange("p h t -> p (h t)")
                dve.tensor_scalar(max_parts[:, 0, :], flat, -1.0, None, ALU.mult).then_inc(max_step, 1)
                dve.wait_ge(max_step, n0 + 3)
                dve.scalar_tensor_tensor(out=maxr[:, :], in0=flat, scalar=-1.0, in1=max_parts[:, 0, :], op0=ALU.mult,
                                         op1=ALU.subtract).then_inc(max_step, 1)
                dve.wait_ge(max_step, n0 + 4)
                dve.tensor_copy(max_parts[:, 1, :], maxr[:, :]).then_inc(max_step, 1)
                dve.wait_ge(max_step, n0 + 5)
                dve.tensor_tensor(max_parts[:, 2, :], maxr[:, :], max_parts[:, 1, :],
                                  ALU.subtract).then_inc(max_parts_done, 1)

            def store_outputs(s, b, ps):
                o = ps[:, :].rearrange("p (t h c) -> p t h c", t=HT, c=VW)
                dve.reciprocal(rsum[:, b, :, :], o[:, :, :, HD]).then_inc(rsum_done, 1)
                dve.wait_ge(rsum_done, s * 2 + (b + 1))
                if isinstance(s, int):
                    dst = attn[:, b * HT:(b + 1) * HT, s * QH * HD:(s + 1) * QH * HD]
                else:
                    dst = attn[:, b * HT:(b + 1) * HT, bass.ds(s * (QH * HD), QH * HD)]
                dve.tensor_tensor(dst.rearrange("p t (h c) -> p t h c", c=HD), o[:, :, :, 0:HD],
                                  rsum[:, b, :, :].unsqueeze(3).to_broadcast([P, HT, QH, HD]),
                                  ALU.mult).then_inc(ring_a_used, 1)

            def step(s, parity, kind):
                k = 0
                for group in steps_of(kind):
                    for use in group:
                        ring_a_use(s, k, parity, use)
                        k += 1

            parity0 = (n_uses(-1) + n_uses(0)) % RING
            step(-1, 0, -1)
            step(0, n_uses(-1) % RING, 0)
            with dve.Fori(0, (NQ - 2) // SLOTS) as i:
                for c in range(SLOTS):
                    step(i * SLOTS + (1 + c), parity0, 1)
            step(NQ - 1, parity0, NQ - 1)
            dve.wait_ge(ring_a_done, last_use)
            store_outputs(NQ - 1, 1, ring_a[(last_use - 1) % RING])

            def attn_rest(t):
                dve.wait_ge(aT_hi_done, t + 1)
                dve.tensor_tensor(aT_lo[:, t % 2, :, :], attnT_ps[t % 2][:, :].rearrange("p (a b) -> p a b", b=P),
                                  aT_hi[:, t % 2, :, :].bitcast(F32), ALU.subtract).then_inc(aT_lo_done, 1)

            attn_rest(0)
            for t in range(NT):
                if t + 1 < NT:
                    attn_rest(t + 1)
                dve.wait_ge(proj_done, t + 1)
                dve.tensor_tensor(x_tok[:, t, :], proj_ps[t % 2][:, :], x_tok[:, t, :], ALU.add).then_inc(x_added, 1)
            ln_norm(4)
            ln_norm(5)
            ln_rest(4)
            ln_rest(5)
            ffn(1, 0)
            ffn(1, 1)



def _bf16_bits(a):
    return (np.ascontiguousarray(a, np.float32).view(np.uint32) >> 16).astype(np.uint16)


def _bf16_parts(a):
    rest, found = np.asarray(a, np.float32), []
    for _ in range(PARTS):
        part = (rest.view(np.uint32) & np.uint32(0xFFFF0000)).view(np.float32)
        found.append(part)
        rest = rest - part
    return found


def _bias_rows():
    slope = (1.0 / np.power(2.0, np.arange(1, H + 1) * (8 / H))).astype(np.float32)
    pos = np.arange(S)
    low = pos % 8
    high = pos - low
    q = np.zeros((H, N_BIAS, S), np.float32)
    k = np.ones((H, N_BIAS + PARTS, S), np.float32)
    for p, s in enumerate(_bf16_parts(slope)):
        for n, where in enumerate((high, low)):
            row = 4 * p + 2 * n
            q[:, row, :], k[:, row, :] = s[:, None], where
            q[:, row + 1, :], k[:, row + 1, :] = where, -s[:, None]
    return [_bf16_bits(a.reshape(NQ, QH, a.shape[1], S).transpose(0, 2, 1, 3)) for a in (q, k)]


def _constants():
    eye = np.eye(P, dtype=np.float32)
    upper = np.triu(np.ones((P, P), np.float32), 1) * np.float32(MASKED)
    bias_q, bias_k = _bias_rows()
    return {"ident": eye, "ident_b": _bf16_bits(eye), "masks": _bf16_bits(np.stack([upper, upper.T], axis=1)),
            "bias_q": bias_q, "bias_k": bias_k}


def kernel(L0_attn_hidden_states, L0_attn_w_qkv, L0_attn_q_ln_w, L0_attn_q_ln_b, L0_attn_k_ln_w, L0_attn_k_ln_b,
           L0_attn_w_out, L0_ffn_W_gate, L0_ffn_W_up, L0_ffn_W_down):
    import concourse.bacc as _bacc
    from concourse.bass_utils import run_bass_kernel_spmd as _run

    f32 = lambda a: np.asarray(a)
    w_ffn = np.zeros((FT, P, FFN_RAW), np.float32)
    for n, w in enumerate((f32(L0_ffn_W_gate), f32(L0_ffn_W_up))):
        padded = np.zeros((FT * P, D), np.float32)
        padded[0:F] = w
        w_ffn[:, :, n * D:(n + 1) * D] = padded.reshape(FT, P, DT, P).transpose(0, 3, 2, 1).reshape(FT, P, D)
    padded = np.zeros((FT * P, D), np.float32)
    padded[0:F] = f32(L0_ffn_W_down).T
    w_ffn[:, :, 2 * D:] = padded.reshape(FT, P, D)
    w_qkv = np.ascontiguousarray(f32(L0_attn_w_qkv).T).reshape(DT, P, 3 * D)
    w_out = f32(L0_attn_w_out).T.reshape(2, 2, P, D).transpose(0, 2, 1, 3).reshape(2, P, 2 * D)
    column = lambda a, b: np.stack([f32(a).reshape(DT, P).T, f32(b).reshape(DT, P).T], axis=1)
    arrays = {
        "x": f32(L0_attn_hidden_states).reshape(S, D),
        "w_ffn": w_ffn,
        "w_qkv": w_qkv,
        "w_out": w_out,
        "ln_w": column(L0_attn_q_ln_w, L0_attn_k_ln_w),
        "ln_b": column(L0_attn_q_ln_b, L0_attn_k_ln_b),
        **_constants(),
    }
    nc = _bacc.Bacc("TRN2", target_bir_lowering=False, num_devices=1)
    args = []
    for name, a in arrays.items():
        arrays[name] = np.ascontiguousarray(a)
        ap = nc.dram_tensor(name, a.shape, mybir.dt.from_np(a.dtype), kind="ExternalInput").ap()
        args.append(ap.bitcast(BF16) if a.dtype == np.uint16 else ap)
    out = nc.dram_tensor("y", (S, D), F32, kind="ExternalOutput").ap()
    x, w_f, w_q, w_o, l_w, l_b, ident, ident_b, masks, bias_q, bias_k = args
    macaron_block(nc, x, w_f, w_q, w_o, l_w, l_b, ident, ident_b, masks, bias_q, bias_k, out)
    r = _run(nc, [arrays], core_ids=[0])
    return r.results[0]["y"].reshape(1, S, D)
```

```python
from contextlib import ExitStack

import numpy as np

import concourse.bass as bass
from concourse import mybir

F32 = mybir.dt.float32
F32R = mybir.dt.float32r
BF16 = mybir.dt.bfloat16
ALU = mybir.AluOpType
ACT = mybir.ActivationFunctionType
AX_X = mybir.AxisListType.X

P = 128
S = 1024
D = 512
F = 1376
H = 32
HD = D // H
NT = S // P
DT = D // P
HALF = S // 2
HT = NT // 2
FT = -(-F // P)
QH = 4
NQ = H // QH
PARTS = 3
CLIP = 8.0
EPS = 1e-5
SCALE = HD ** -0.5
MASKED = -1e30

Q_RUNS = ((0, 3), (0, 2), (0, 1))
K_RUNS = ((0, 1), (0, 1), (0, 1), (1, 1), (1, 1), (2, 1))
N_PAIRS = 6
ROW_BIAS = N_PAIRS * HD
N_BIAS = 4 * PARTS
ROW_MAX = ROW_BIAS + N_BIAS
N_ROWS = ROW_MAX + PARTS
VC = HD + 1
VW = 32
SLOTS = 3
RING = 3

FFN_RAW = 3 * D

RAW_FFN = (0, 2 * FT)
PAIRS = (FT - 3) // 2
assert PAIRS == DT

LN_INSIDE = {(0, 0): 1, (0, 1): 2, (1, 0): 5}

MAX_CHUNKS = []
for _t in range(NT):
    for _j in range(_t // HT + 1):
        _diag = _t // HT == _j
        MAX_CHUNKS.append((_t, _j, (_t % HT + 1) * P if _diag else HALF, (_t % HT) * P if _diag else None))
KEY_GROUPS = [(b, kt, max(b * HALF, kt * P), kt // HT == b) for b in range(2) for kt in range((b + 1) * HT)]
NC = len(MAX_CHUNKS)
NG = len(KEY_GROUPS)
HALF_END = (HT - 1, NG - 1)


LAG = 6


def groups_of(s):
    return [p - LAG for p in range(NG) if (s > 0 or p >= LAG) and (s < NQ or p < LAG)]


def steps_of(s):
    uses = [[[] for _ in range(QH)] for _ in range(NG)]
    width = [(b + 1) * HALF - q0 for b, kt, q0, diag in KEY_GROUPS]
    work = [0.25 + (2 * width[p - LAG] + 3 * width[p - LAG - 1]) / HALF / 5 for p in range(NG)]
    if s < NQ - 1:
        chunks = [("max", (h, c)) for h in range(QH) for c in range(NC)]
        sizes = [0.2 + MAX_CHUNKS[c][2] / HALF for _, (h, c) in chunks]
        first = LAG if s == 0 else 0
        places, done, given = sum(work[first:]), 0, 0
        for p in range(first, NG):
            for h in range(QH):
                done += work[p] / QH
                while chunks and given + sizes[0] / 2 < done / places * sum_sizes(sizes, given):
                    uses[p][h].append(chunks.pop(0))
                    given += sizes.pop(0)
        uses[NG - 1][QH - 1] += chunks
    if 0 <= s < NQ:
        p = LAG if s == 0 else MAX_PLACE
        uses[p][0].insert(0, ("maxT", None))
    if s > 0:
        uses[OUT_PLACE[0]][1].append(("out", 0))
        uses[OUT_PLACE[1]][0].append(("out", 1))
    return uses


def sum_sizes(left, given):
    return sum(left) + given


OUT_PLACE = {1: LAG + 2, 0: (LAG + HT + 2) % NG}
MAX_PLACE = 1


def n_uses(s):
    return sum(len(uses) for place in steps_of(s) for uses in place)


def use_base(s):
    first = n_uses(-1)
    if isinstance(s, int) and s < 0:
        return 0
    if isinstance(s, int) and s == 0:
        return first
    if isinstance(s, int) and s == NQ:
        return use_base(NQ - 1) + n_uses(NQ - 1)
    return (s - 1) * n_uses(1) + (first + n_uses(0))


def macaron_block(nc, x_in, w_ffn, w_qkv, w_out, ln_w, ln_b, ident_in, ident_b_in, mask_in, bias_q, bias_k, out):
    ctx = ExitStack()
    with ctx:
        at = [-(-nc.sbuf_base // 64) * 64]

        def place(name, shape, dt, offset=None):
            size = int(np.prod(shape[1:])) * (2 if dt == BF16 else 4)
            if offset is None:
                offset, at[0] = at[0], -(-(at[0] + size) // 64) * 64
            return nc.alloc_sbuf_tensor_at(name, shape, dt, offset=offset)

        def region(size):
            start, at[0] = at[0], at[0] + size
            return start

        def sem(name):
            return ctx.enter_context(nc.semaphore(name))

        KB = 1024
        x_tok = place("x_tok", [P, NT, D], F32)
        xnT_at = region(32 * KB)
        xnT_hi = place("xnT_hi", [P, DT, S], F32R, xnT_at)
        xnT_lo = place("xnT_lo", [P, DT, S], F32R, xnT_at + 16 * KB)
        raw = place("raw", [P, 2, FFN_RAW], F32)
        xn = place("xn", [P, HT, D], F32)
        v_aug = place("v_aug", [P, NT, H * VC + HD], F32)
        ident = place("ident", [P, P], F32)
        ident_b = place("ident_b", [P, P], BF16)
        masks = place("masks", [P, 2, P], BF16)
        lnw = place("lnw", [P, 2, DT], F32)
        lnb = place("lnb", [P, 2, DT], F32)
        ln_stat = place("ln_stat", [P, 2, HT, 6], F32)
        ln_mv = place("ln_mv", [P, 2, HT, 2], F32)
        ln_var = place("ln_var", [P, 2, HT], F32)
        ln_rstd = place("ln_rstd", [P, 2, HT], F32)
        minus_half = place("minus_half", [P, HT], F32)
        qk_stat = place("qk_stat", [P, 2, 2, 6], F32)
        qk_mv = place("qk_mv", [P, 2, 2, 2], F32)
        qk_var = place("qk_var", [P, 2, 2], F32)
        qk_rstd = place("qk_rstd", [P, 2, 2], F32)
        A = region(40 * KB)
        gu_hi = place("gu_hi", [P, 2, 2, DT, P], F32R, A)
        gu_lo = place("gu_lo", [P, 2, 2, DT, P], F32R, A + 8 * KB)
        dn_hi = place("dn_hi", [P, 2, D], F32R, A + 16 * KB)
        dn_lo = place("dn_lo", [P, 2, D], F32R, A + 20 * KB)
        silu = place("silu", [P, 2, HALF], F32, A + 24 * KB)
        hid = place("hid", [P, 2, HALF], F32, A + 28 * KB)
        hid_hi = place("hid_hi", [P, 2, HALF], F32R, A + 32 * KB)
        hid_lo = place("hid_lo", [P, 2, HALF], F32R, A + 36 * KB)
        parts = place("parts", [P, 2, DT, 2, PARTS, 2 * P], BF16, A)
        attn = place("attn", [P, NT, D], F32, A)
        oT = place("oT", [P, 2, HALF], F32, A + 16 * KB)
        maxp = place("maxp", [P, QH, NC], F32, A + 20 * KB)
        maxv = place("maxv", [P, QH, NT], F32, A + 20 * KB + 512)
        maxr = place("maxr", [P, QH * NT], F32, A + 21 * KB)
        max_parts = place("max_parts", [P, PARTS, QH * NT], BF16, A + 21 * KB + 512)
        maxT = place("maxT", [PARTS * QH * NT, P], BF16, A + 22 * KB)
        rsum = place("rsum", [P, 2, HT, QH], F32, A + 23 * KB)
        wout_hi = place("wout_hi", [P, DT, D], F32R, A + 24 * KB)
        wout_lo = place("wout_lo", [P, DT, D], F32R, A + 32 * KB)
        B = region(72 * KB)
        wqk_hi = place("wqk_hi", [P, DT, 2 * D], F32R, B)
        wqk_lo = place("wqk_lo", [P, DT, 2 * D], F32R, B + 16 * KB)
        wv_hi = place("wv_hi", [P, DT, D], F32R, B + 32 * KB)
        wv_lo = place("wv_lo", [P, DT, D], F32R, B + 40 * KB)
        raw_qkv = place("raw_qkv", [P, DT, 3 * D], F32, B + 48 * KB)
        qk = place("qk", [P, 2, 2, D], F32, B + 48 * KB)
        qkT = place("qkT", [P, 2, 2, DT, P], F32, B + 56 * KB)
        qkT_rest = place("qkT_rest", [P, 2, 2, DT, P], F32, B + 64 * KB)
        rows = place("rows", [P, SLOTS, 2, QH, S], BF16, B)
        q_rows, k_rows = rows[:, :, 0], rows[:, :, 1]
        probs = place("probs", [P, 3, QH, HALF], F32, B + 48 * KB)
        v_quad = place("v_quad", [P, SLOTS, NT, QH * VC + HD], F32, xnT_at)
        aT_hi = place("aT_hi", [P, 2, DT, P], F32R, B)
        aT_lo = place("aT_lo", [P, 2, DT, P], F32R, B + 4 * KB)

        bank = [ctx.enter_context(nc.psum_tensor(f"bank{i}", [P, 512], F32)) for i in range(8)]
        gate_ps, up_ps, y_ps = bank[0:2], bank[2:4], bank[4:8]
        lnT_ps = {0: bank[0:4], 3: bank[4:6], 4: bank[0:4]}
        for l in LN_INSIDE.values():
            lnT_ps[l] = y_ps
        qk_ps, v_ps, qkT_ps = [bank[0:2], bank[2:4]], bank[4:6], bank[6:8]
        ring_a, ring_b, o_ps = bank[0:3], bank[3:6], bank[6:8]
        proj_ps, attnT_ps = bank[4:6], bank[6:8]

        qk_scr = nc.dram_tensor("qk_scr", (DT, 2, PARTS, P, S), BF16, kind="Internal").ap()
        max_scr = nc.dram_tensor("max_scr", (2, PARTS, QH * S), BF16, kind="Internal").ap()

        ident_loaded = sem("ident_loaded")
        const_in = sem("const_in")
        x_loaded = [sem(f"x_loaded{i}") for i in range(NT)]
        raw_in = [sem(f"raw_in{i}") for i in range(2)]
        raw_qkv_in = sem("raw_qkv_in")
        raw_out_in = sem("raw_out_in")
        w_hi = sem("w_hi")
        w_lo = sem("w_lo")
        wqkv_hi_done = sem("wqkv_hi_done")
        wqkv_lo_done = sem("wqkv_lo_done")
        wout_hi_done = sem("wout_hi_done")
        wout_lo_done = sem("wout_lo_done")
        half_set = sem("half_set")
        q_scaled = sem("q_scaled")
        v_ones = sem("v_ones")
        ln_stats = sem("ln_stats")
        ln_mean = sem("ln_mean")
        ln_eps = sem("ln_eps")
        ln_rs = sem("ln_rs")
        ln_normed = sem("ln_normed")
        ln_turned = sem("ln_turned")
        ln_hi = sem("ln_hi")
        ln_lo = sem("ln_lo")
        gate_done = sem("gate_done")
        up_done = sem("up_done")
        down_done = sem("down_done")
        y_done = sem("y_done")
        silu_done = sem("silu_done")
        hid_done = sem("hid_done")
        hid_hi_done = sem("hid_hi_done")
        hid_lo_done = sem("hid_lo_done")
        x_added = sem("x_added")
        qk_done = sem("qk_done")
        v_done = sem("v_done")
        clipped = sem("clipped")
        v_clipped = sem("v_clipped")
        qk_stats = sem("qk_stats")
        qk_mean = sem("qk_mean")
        qk_eps = sem("qk_eps")
        qk_rs = sem("qk_rs")
        qk_normed = sem("qk_normed")
        qk_turned = sem("qk_turned")
        qkT_done = sem("qkT_done")
        part0_done = sem("part0_done")
        rest1_done = sem("rest1_done")
        part1_done = sem("part1_done")
        part2_done = sem("part2_done")
        parts_out = [sem(f"parts_out{i}") for i in range(2)]
        rows_in = [sem(f"rows_in{i}") for i in range(SLOTS)]
        v_in = [sem(f"v_in{i}") for i in range(SLOTS)]
        max_out = sem("max_out")
        max_in = [sem(f"max_in{i}") for i in range(SLOTS)]
        ring_a_done = sem("ring_a_done")
        ring_a_used = sem("ring_a_used")
        ring_b_done = sem("ring_b_done")
        probs_done = sem("probs_done")
        pv_done = sem("pv_done")
        oT_done = sem("oT_done")
        max_step = sem("max_step")
        max_parts_done = sem("max_parts_done")
        rsum_done = sem("rsum_done")
        attn_turned = sem("attn_turned")
        aT_hi_done = sem("aT_hi_done")
        aT_lo_done = sem("aT_lo_done")
        proj_done = sem("proj_done")
        out_sent = sem("out_sent")

        def atleast(eng, s, value):
            if not isinstance(value, int) or value > 0:
                eng.wait_ge(s, value)

        def wait_down(eng, half, k):
            if not isinstance(k, int) or k >= 2:
                eng.wait_ge(down_done, k + ((FT - 1) * half - 1))
            elif half and k == 0:
                eng.wait_ge(down_done, (FT - 1) * half)
            elif half:
                eng.wait_ge(y_done, HT * half)

        def wait_raw(eng, r0, k, parity):
            eng.wait_ge(raw_in[(r0 + parity) % 2], (k + (r0 - (r0 + parity) % 2 + 2)) * 8)

        def lnT_bank(l, t):
            return lnT_ps[l][t % len(lnT_ps[l])]

        last_use = use_base(NQ) + n_uses(NQ)

        def use_of(s, use):
            k = 0
            for place in steps_of(s if isinstance(s, int) else 1):
                for uses in place:
                    for this in uses:
                        k += 1
                        if this == use:
                            return use_base(s) + k
            raise ValueError(use)

        constants = ((ident_b, ident_b_in), (masks, mask_in), (lnw, ln_w), (lnb, ln_b))
        LN_BEHIND = NT - 1 - HT
        block = ctx.enter_context(nc.Block())

        @block.sync
        def _(sp):
            def load_x(t):
                sp.dma_start(x_tok[:, t, :], x_in[t * P:(t + 1) * P, :]).then_inc(x_loaded[t], 16)

            def load_raw(r, parity, src, width):
                atleast(sp, w_hi, 2 * r - 2)
                atleast(sp, w_lo, 2 * r - 2)
                sp.dma_start(raw[:, parity, 0:width], src).then_inc(raw_in[parity], 16)

            def load_first(n):
                load_raw(RAW_FFN[n], RAW_FFN[n] % 2, w_ffn[0], FFN_RAW)

            def load_ffn(n):
                for b in range(2):
                    r0 = RAW_FFN[n] + b * FT
                    if b:
                        load_raw(r0, r0 % 2, w_ffn[0], FFN_RAW)
                    with sp.Fori(0, (FT - 1) // 2) as i:
                        for c in range(2):
                            load_raw(i * 2 + (r0 + 1 + c), (r0 + 1 + c) % 2, w_ffn[i * 2 + (1 + c)], FFN_RAW)
                    if n == 0 and b == 0:
                        sp.dma_start(raw_qkv[:, :, :], w_qkv).then_inc(raw_qkv_in, 16)

            for t in range(HT):
                load_x(t)
            sp.dma_start(ident[:, :], ident_in).then_inc(ident_loaded, 16)
            load_first(0)
            for t in range(HT, NT):
                load_x(t)
            for dst, src in constants:
                sp.dma_start(dst[tuple(slice(None) for _ in src.shape)], src).then_inc(const_in, 16)
            load_ffn(0)
            load_first(1)
            sp.wait_ge(ln_turned, HT * 4)
            sp.dma_start(xn[:, :, :], w_out).then_inc(raw_out_in, 16)

            for j in range(NT // 2):
                sp.wait_ge(part2_done, 2 * j + 2)
                sp.dma_start(qk_scr.rearrange("n c p r t -> r (n c p) t")[:, :, j * 2 * P:(j + 1) * 2 * P],
                             parts[:, j % 2].rearrange("r n c p t -> r (n c p) t")).then_inc(parts_out[j % 2], 16)
            for j in range(2):
                sp.wait_ge(parts_out[j], 16 * NT // 4)

            def load_rows(g):
                slot, n, heads = g % SLOTS, g * QH * HD // P, slice(g * QH % (P // HD), g * QH % (P // HD) + QH)
                for c, runs in ((0, Q_RUNS), (1, K_RUNS)):
                    row = 0
                    for part, length in runs:
                        src = qk_scr[n, c, part:part + length].rearrange("p (d h) t -> (p d) h t", d=HD)[:, heads, :]
                        sp.dma_start(rows[row:row + length * HD, slot, c, :, :], src).then_inc(rows_in[slot], 16)
                        row += length * HD
                sp.dma_start(rows[ROW_BIAS:ROW_MAX, slot, 0, :, :], bias_q[g]).then_inc(rows_in[slot], 16)
                sp.dma_start(rows[ROW_BIAS:N_ROWS, slot, 1, :, :], bias_k[g]).then_inc(rows_in[slot], 16)

            def load_v(g):
                sp.dma_start(v_quad[:, g % SLOTS, :, :],
                             v_aug[:, :, g * QH * VC:(g + 1) * QH * VC + HD]).then_inc(v_in[g % SLOTS], 16)

            def move_max(g):
                sp.wait_ge(ring_a_used, use_of(g, ("maxT", None)))
                if g >= 2:
                    sp.wait_ge(max_in[(g - 2) % SLOTS], 16 * ((g - 2) // SLOTS + 1))
                sp.dma_start(max_scr[g % 2].rearrange("p (r c) -> (p r) c", c=P), maxT[:, :]).then_inc(max_out, 16)
                sp.wait_ge(max_out, 16 * (g + 1))
                sp.dma_start(q_rows[ROW_MAX:N_ROWS, g % SLOTS, :, :],
                             max_scr[g % 2].rearrange("p (h t) -> p h t", h=QH)).then_inc(max_in[g % SLOTS], 16)

            load_rows(0)
            load_rows(1)
            sp.wait_ge(v_clipped, NT)
            for g in range(SLOTS - 1):
                load_v(g)
            for s in range(NQ):
                move_max(s)
                if s + 2 < NQ:
                    if s > 0:
                        sp.wait_ge(pv_done, NG * s)
                    load_rows(s + 2)
                    load_v(s + 2)

            load_ffn(1)
            for t in range(NT):
                sp.wait_ge(x_added, 2 * NT + t + 1)
                sp.dma_start(out[t * P:(t + 1) * P, :], x_tok[:, t, :]).then_inc(out_sent, 16)
            sp.wait_ge(out_sent, 16 * NT)

        @block.gpsimd
        def _(pool):
            pool.memset(minus_half[:, :], -0.5).then_inc(half_set, 1)
            pool.wait_ge(half_set, 1)

            def rsqrt(mv_ready, count, mv, var, rstd, eps_sem, rs_sem, done):
                pool.wait_ge(mv_ready, count)
                pool.tensor_scalar(var, mv, EPS, None, ALU.add).then_inc(eps_sem, 1)
                pool.wait_ge(eps_sem, done)
                pool.tensor_tensor(rstd, var, minus_half[:, 0:var.shape[1]], ALU.pow).then_inc(rs_sem, 1)

            def ln(l):
                b = l % 2
                for t in range(HT):
                    n = HT * l + t + 1
                    rsqrt(ln_mean, n, ln_mv[:, b, t, 1:2], ln_var[:, b, t:t + 1], ln_rstd[:, b, t:t + 1],
                          ln_eps, ln_rs, n)

            ln(0)
            pool.wait_ge(const_in, 16 * len(constants))
            for a in (lnw, lnb):
                pool.tensor_scalar(a[:, 0, :], a[:, 0, :], SCALE, None, ALU.mult).then_inc(q_scaled, 1)
            pool.memset(v_aug[:, :, :], 1.0).then_inc(v_ones, 1)
            for l in range(1, 4):
                ln(l)
            for t in range(NT):
                rsqrt(qk_mean, t + 1, qk_mv[:, t % 2, :, 1], qk_var[:, t % 2, :], qk_rstd[:, t % 2, :],
                      qk_eps, qk_rs, t + 1)
            for l in range(4, 6):
                ln(l)

        @block.tensor
        def _(pe):
            def three_pass(dst, a_hi, a_lo, b_hi, b_lo, start, stop):
                pe.matmul(dst, a_hi, b_hi, start=start, stop=False)
                pe.matmul(dst, a_hi, b_lo, start=False, stop=False)
                return pe.matmul(dst, a_lo, b_hi, start=False, stop=stop)

            def ln_turn(l, t):
                n, ps = HT * l + t, lnT_bank(l, t)
                pe.wait_ge(ln_normed, n + 1)
                if t >= len(lnT_ps[l]):
                    pe.wait_ge(ln_lo, n + 1 - len(lnT_ps[l]))
                for dt in range(DT):
                    ins = pe.transpose(ps[:, dt * P:(dt + 1) * P], xn[:, t, dt * P:(dt + 1) * P], ident[:, :])
                ins.then_inc(ln_turned, 1)

            def ffn(n, b):
                r0, k0, inside = RAW_FFN[n] + b * FT, (2 * n + b) * FT, LN_INSIDE.get((n, b))
                tok = slice(b * HALF, (b + 1) * HALF)

                def gate_up(k, parity):
                    slot = (k0 + parity) % 2
                    pe.wait_ge(w_hi, k * 2 + (2 * r0 + 1))
                    pe.wait_ge(w_lo, k * 2 + (2 * r0 + 1))
                    for which, ps, freed, done in ((0, gate_ps, silu_done, gate_done), (1, up_ps, hid_done, up_done)):
                        atleast(pe, freed, k + (k0 - 1))
                        for dt in range(DT):
                            ins = three_pass(ps[slot][:, :], gu_hi[:, slot, which, dt, :], gu_lo[:, slot, which, dt, :],
                                             xnT_hi[:, dt, tok], xnT_lo[:, dt, tok], dt == 0, dt == DT - 1)
                        ins.then_inc(done, 1)

                def down(k, parity, first=False, last=False):
                    slot = (k0 + parity) % 2
                    pe.wait_ge(w_hi, k * 2 + (2 * r0 + 2))
                    pe.wait_ge(w_lo, k * 2 + (2 * r0 + 2))
                    pe.wait_ge(hid_lo_done, k + (k0 + 1))
                    for t in range(HT):
                        if first and inside:
                            pe.wait_ge(ln_lo, HT * inside + t + 1)
                        elif first:
                            pe.wait_ge(x_added, NT * (2 * n) + t + 1)
                        cols = slice(t * P, (t + 1) * P)
                        ins = three_pass(y_ps[t][:, :], hid_hi[:, slot, cols], hid_lo[:, slot, cols],
                                         dn_hi[:, slot, :], dn_lo[:, slot, :], first, last)
                        if last:
                            ins.then_inc(y_done, 1)
                    if not last:
                        ins.then_inc(down_done, 1)

                pe.wait_ge(ln_lo, HT * (4 * n + b + 1))
                gate_up(0, 0)
                gate_up(1, 1)
                if inside:
                    for t in range(HT):
                        ln_turn(inside, t)
                down(0, 0, first=True)
                with pe.Fori(0, PAIRS) as i:
                    gate_up(i * 2 + 2, 0)
                    down(i * 2 + 1, 1)
                    gate_up(i * 2 + 3, 1)
                    down(i * 2 + 2, 0)
                gate_up(FT - 1, 0)
                down(FT - 2, 1)
                down(FT - 1, 0, last=True)

            pe.wait_ge(ident_loaded, 16)
            for t in range(HT):
                ln_turn(0, t)
            ffn(0, 0)
            ffn(0, 1)

            def project_qk(t):
                if t == 0:
                    pe.wait_ge(wqkv_hi_done, 2 * DT)
                    pe.wait_ge(wqkv_lo_done, 2 * DT)
                if t < HT:
                    pe.wait_ge(ln_lo, HT * 3)
                else:
                    pe.wait_ge(ln_lo, HT * 3 + t - HT + 1)
                cols = slice(t * P, (t + 1) * P)
                for c in range(2):
                    atleast(pe, clipped, 2 * (t - 2) + c + 1)
                    for dt in range(DT):
                        w = slice(c * D, (c + 1) * D)
                        ins = three_pass(qk_ps[t % 2][c][:, :], xnT_hi[:, dt, cols], xnT_lo[:, dt, cols],
                                         wqk_hi[:, dt, w], wqk_lo[:, dt, w], dt == 0, dt == DT - 1)
                    ins.then_inc(qk_done, 1)

            def project_v(t):
                cols = slice(t * P, (t + 1) * P)
                atleast(pe, v_clipped, t - 1)
                for dt in range(DT):
                    ins = three_pass(v_ps[t % 2][:, :], xnT_hi[:, dt, cols], xnT_lo[:, dt, cols],
                                     wv_hi[:, dt, :], wv_lo[:, dt, :], dt == 0, dt == DT - 1)
                ins.then_inc(v_done, 1)

            def qk_turn(t):
                pe.wait_ge(qk_normed, t + 1)
                atleast(pe, qkT_done, t)
                for c in range(2):
                    for dt in range(DT):
                        ins = pe.transpose(qkT_ps[c][:, dt * P:(dt + 1) * P], qk[:, t % 2, c, dt * P:(dt + 1) * P],
                                           ident[:, :])
                ins.then_inc(qk_turned, 1)

            for t in range(NT):
                project_qk(t)
                if 0 < t <= HT // 2:
                    for c in range(2):
                        ln_turn(3, 2 * (t - 1) + c)
                if t == HT // 2 + 1:
                    pe.wait_ge(const_in, 16 * len(constants))
                if t > 0:
                    qk_turn(t - 1)
            for t in range(NT):
                if t == 1:
                    qk_turn(NT - 1)
                project_v(t)

            def ring_a_use(s, k, parity, use, slot, next_slot):
                kind, what = use
                ps = ring_a[(parity + k) % RING]
                atleast(pe, ring_a_used, use_base(s) + (k + 1 - RING))
                if kind == "max":
                    h, c = what
                    t, j, width, diag = MAX_CHUNKS[c]
                    ins = pe.matmul(ps[:, 0:width], q_rows[0:ROW_MAX, next_slot, h, t * P:(t + 1) * P],
                                    k_rows[0:ROW_MAX, next_slot, h, j * HALF:j * HALF + width],
                                    start=True, stop=diag is None)
                    if diag is not None:
                        ins = pe.matmul(ps[:, diag:diag + P], ident_b[:, :], masks[:, 0, :], start=False, stop=True)
                elif kind == "out":
                    b = what
                    pe.wait_ge(oT_done, s * 2 + (b - 1))
                    for t in range(HT):
                        ins = pe.transpose(ps[:, t * P:(t + 1) * P], oT[:, b, t * P:(t + 1) * P], ident[:, :])
                else:
                    pe.wait_ge(max_parts_done, s + 1)
                    ins = pe.transpose(ps[0:PARTS * QH * NT, 0:P // 2].bitcast(BF16),
                                       max_parts[:, :, :].rearrange("p a b -> p (a b)"), ident_b[:, :])
                ins.then_inc(ring_a_done, 1)

            def scores(s, u, h, slot):
                b, kt, q0, diag = KEY_GROUPS[u % NG]
                width = (b + 1) * HALF - q0
                ps = ring_b[(QH * u + h) % RING]
                atleast(pe, probs_done, s * (NG * QH) + (QH * u + h + 1 - RING))
                args = (ps[:, 0:width], k_rows[0:N_ROWS, slot, h, kt * P:(kt + 1) * P],
                        q_rows[0:N_ROWS, slot, h, q0:q0 + width])
                ins = pe.matmul(*args, start=True, stop=not diag)
                if diag:
                    ins = pe.matmul(ps[:, 0:P], ident_b[:, :], masks[:, 1, :], start=False, stop=True)
                ins.then_inc(ring_b_done, 1)

            def values(s, u, slot):
                b, kt, q0, diag = KEY_GROUPS[u % NG]
                pe.wait_ge(probs_done, s * (NG * QH) + QH * (u + 1))
                if kt == 0:
                    atleast(pe, oT_done, s * 2 + (b - 1 + 2 * (u // NG)))
                for h in range(QH):
                    ins = pe.matmul(o_ps[b][VW * h:VW * (h + 1), q0 - b * HALF:HALF],
                                    v_quad[:, slot, kt, h * VC:h * VC + VW], probs[:, u % 3, h, 0:(b + 1) * HALF - q0],
                                    start=kt == 0, stop=u % NG in HALF_END)
                ins.then_inc(pv_done, 1)

            def step(s, slot, parity, kind):
                next_slot = (slot + 1) % SLOTS
                if kind < NQ - 1:
                    rows_wait(s, next_slot, kind)
                k = 0
                for p, place in enumerate(steps_of(kind)):
                    u = p - LAG
                    active = kind >= 0 and u in groups_of(kind)
                    for h in range(QH):
                        for use in place[h]:
                            ring_a_use(s, k, parity, use, slot, next_slot)
                            k += 1
                        if active:
                            if u == 0 and h == 0:
                                max_wait(s, slot)
                            scores(s, u, h, (slot if u >= 0 else slot - 1) % SLOTS)
                    if kind > 0 and (u - 1 in groups_of(kind) or u - 1 == -LAG - 1) or kind == 0 and u > 0:
                        if u == 1 and kind < NQ:
                            v_wait(s, slot)
                        values(s, u - 1, (slot if u > 0 else slot - 1) % SLOTS)

            n_rows_dma = len(Q_RUNS) + len(K_RUNS) + 2

            def rows_wait(s, next_slot, kind):
                if isinstance(s, int):
                    pe.wait_ge(rows_in[next_slot], 16 * n_rows_dma * ((s + 1) // SLOTS + 1))
                else:
                    pe.wait_ge(rows_in[next_slot], loop_turn[0] * (16 * n_rows_dma) + 16 * n_rows_dma * loop_turn[1])

            def max_wait(s, slot):
                if isinstance(s, int):
                    pe.wait_ge(max_in[slot], 16 * (s // SLOTS + 1))
                else:
                    pe.wait_ge(max_in[slot], loop_turn[0] * 16 + 16 * loop_turn[2])

            def v_wait(s, slot):
                if isinstance(s, int):
                    pe.wait_ge(v_in[slot], 16 * (s // SLOTS + 1))
                else:
                    pe.wait_ge(v_in[slot], loop_turn[0] * 16 + 16 * loop_turn[2])

            loop_turn = [None, 0, 0]
            parity0 = (n_uses(-1) + n_uses(0)) % RING
            assert n_uses(1) % RING == 0
            step(-1, SLOTS - 1, 0, -1)
            step(0, 0, n_uses(-1) % RING, 0)
            with pe.Fori(0, (NQ - 2) // SLOTS) as i:
                for c in range(SLOTS):
                    loop_turn[:] = [i, (2 + c) // SLOTS + 1, (1 + c) // SLOTS + 1]
                    step(i * SLOTS + (1 + c), (1 + c) % SLOTS, parity0, 1)
            step(NQ - 1, (NQ - 1) % SLOTS, parity0, NQ - 1)
            step(NQ, NQ % SLOTS, use_base(NQ) % RING, NQ)

            def attn_turn(t):
                pe.wait_ge(ring_a_used, last_use)
                atleast(pe, aT_lo_done, t - 1)
                for dt in range(DT):
                    ins = pe.transpose(attnT_ps[t % 2][:, dt * P:(dt + 1) * P], attn[:, t, dt * P:(dt + 1) * P],
                                       ident[:, :])
                ins.then_inc(attn_turned, 1)

            def out_project(t):
                pe.wait_ge(aT_lo_done, t + 1)
                atleast(pe, x_added, NT + t - 1)
                for dt in range(DT):
                    ins = three_pass(proj_ps[t % 2][:, :], aT_hi[:, t % 2, dt, :], aT_lo[:, t % 2, dt, :],
                                     wout_hi[:, dt, :], wout_lo[:, dt, :], dt == 0, dt == DT - 1)
                ins.then_inc(proj_done, 1)

            pe.wait_ge(wout_hi_done, 1)
            pe.wait_ge(wout_lo_done, 1)
            attn_turn(0)
            for t in range(NT):
                if t + 1 < NT:
                    attn_turn(t + 1)
                out_project(t)
                if 0 <= t - LN_BEHIND < HT:
                    ln_turn(4, t - LN_BEHIND)
            ffn(1, 0)
            ffn(1, 1)

        @block.scalar
        def _(act):
            def ln_round(l, t):
                b, n = l % 2, HT * l + t
                cols = slice((b * HT + t) * P, (b * HT + t + 1) * P)
                act.wait_ge(ln_turned, n + 1)
                act.activation(xnT_hi[:, :, cols], lnT_bank(l, t)[:, :].rearrange("p (a b) -> p a b", b=P),
                               ACT.Copy).then_inc(ln_hi, 1)

            def hi_of(dst, src):
                act.activation(dst, src, ACT.Copy).then_inc(w_hi, 1)

            def ffn(n, b):
                r0, k0 = RAW_FFN[n] + b * FT, (2 * n + b) * FT

                def round_gate_up(k, parity):
                    slot, rs = (k0 + parity) % 2, (r0 + parity) % 2
                    wait_raw(act, r0, k, parity)
                    atleast(act, up_done, k + (k0 - 1))
                    hi_of(gu_hi[:, slot, :, :, :].rearrange("p a b c -> p (a b c)"), raw[:, rs, 0:2 * D])

                def round_down(k, parity):
                    slot, rs = (k0 + parity) % 2, (r0 + parity) % 2
                    wait_down(act, 2 * n + b, k)
                    hi_of(dn_hi[:, slot, :], raw[:, rs, 2 * D:])

                def step(k, parity, more=True):
                    slot = (k0 + parity) % 2
                    if more:
                        round_gate_up(k + 1, 1 - parity)
                    act.wait_ge(gate_done, k + (k0 + 1))
                    atleast(act, hid_done, k + (k0 - 1))
                    act.activation(silu[:, slot, :], gate_ps[slot][:, :], ACT.Silu).then_inc(silu_done, 1)
                    act.wait_ge(hid_done, k + (k0 + 1))
                    wait_down(act, 2 * n + b, k)
                    act.activation(hid_hi[:, slot, :], hid[:, slot, :], ACT.Copy).then_inc(hid_hi_done, 1)
                    if more:
                        round_down(k + 1, 1 - parity)

                if b == 0:
                    round_gate_up(0, 0)
                    if n == 0:
                        for t in range(HT):
                            ln_round(0, t)
                    round_down(0, 0)
                step(0, 0)
                if (n, b) in LN_INSIDE:
                    for t in range(HT):
                        ln_round(LN_INSIDE[n, b], t)
                step(1, 1)
                with act.Fori(0, PAIRS) as i:
                    step(i * 2 + 2, 0)
                    step(i * 2 + 3, 1)
                    if (n, b) == (0, 1):
                        act.wait_ge(raw_qkv_in, 16)
                        for dst, cols in ((wqk_hi, slice(0, 2 * D)), (wv_hi, slice(2 * D, 3 * D))):
                            act.activation(dst[:, bass.ds(i, 1), :], raw_qkv[:, bass.ds(i, 1), cols],
                                           ACT.Copy).then_inc(wqkv_hi_done, 1)
                step(FT - 1, 0, more=b == 0)

            ffn(0, 0)
            ffn(0, 1)
            act.wait_ge(q_scaled, 2)
            for t in range(NT):
                slot, pair, cols = t % 2, (t // 2) % 2, slice((t % 2) * P, (t % 2 + 1) * P)
                if t < HT // 2:
                    for c in range(2):
                        ln_round(3, 2 * t + c)
                act.wait_ge(qk_turned, t + 1)
                atleast(act, rest1_done, t - 1)
                for c in range(2):
                    for dt in range(DT):
                        ins = act.activation(qkT[:, slot, c, dt, :], qkT_ps[c][:, dt * P:(dt + 1) * P], ACT.Identity,
                                             bias=lnb[:, c, dt:dt + 1], scale=lnw[:, c, dt:dt + 1])
                ins.then_inc(qkT_done, 1)
                act.wait_ge(qkT_done, t + 1)
                if t % 2 == 0 and t >= 4:
                    act.wait_ge(parts_out[pair], 16)
                for c in range(2):
                    ins = act.activation(parts[:, pair, :, c, 0, cols], qkT[:, slot, c, :, :], ACT.Copy)
                ins.then_inc(part0_done, 1)
                act.wait_ge(rest1_done, t + 1)
                for c in range(2):
                    ins = act.activation(parts[:, pair, :, c, 1, cols], qkT_rest[:, slot, c, :, :], ACT.Copy)
                ins.then_inc(part1_done, 1)

            act.wait_ge(raw_out_in, 16)
            act.activation(wout_hi[:, :, :], xn[:, :, :], ACT.Copy).then_inc(wout_hi_done, 1)

            def read_outputs(s, b):
                act.wait_ge(pv_done, s * NG + (HALF_END[b] + 1))
                if not (isinstance(s, int) and s == 0):
                    act.wait_ge(ring_a_done, use_of(s, ("out", b)))
                act.activation(oT[:, b, :], o_ps[b][:, :], ACT.Copy).then_inc(oT_done, 1)

            def step(s, kind):
                for u in groups_of(kind):
                    b, kt, q0, diag = KEY_GROUPS[u % NG]
                    width = (b + 1) * HALF - q0
                    atleast(act, pv_done, s * NG + (u - 2))
                    for h in range(QH):
                        act.wait_ge(ring_b_done, s * (NG * QH) + (QH * u + h + 1))
                        act.activation(probs[:, u % 3, h, 0:width], ring_b[(QH * u + h) % RING][:, 0:width],
                                       ACT.Exp).then_inc(probs_done, 1)
                    if u == 0 and kind > 0:
                        read_outputs(s - 1, 1)
                    if u == HALF_END[0] + 1:
                        read_outputs(s, 0)

            step(0, 0)
            with act.Fori(0, (NQ - 2) // SLOTS) as i:
                for c in range(SLOTS):
                    step(i * SLOTS + (1 + c), 1)
            step(NQ - 1, NQ - 1)
            step(NQ, NQ)
            read_outputs(NQ - 1, 1)

            def attn_round(t):
                act.wait_ge(attn_turned, t + 1)
                atleast(act, proj_done, t - 1)
                act.activation(aT_hi[:, t % 2, :, :], attnT_ps[t % 2][:, :].rearrange("p (a b) -> p a b", b=P),
                               ACT.Copy).then_inc(aT_hi_done, 1)

            attn_round(0)
            for t in range(NT):
                if t + 1 < NT:
                    attn_round(t + 1)
                if 0 <= t - LN_BEHIND < HT:
                    ln_round(4, t - LN_BEHIND)
            ffn(1, 0)
            ffn(1, 1)

        @block.vector
        def _(dve):
            def ln_stat_of(l, t):
                b = l % 2
                if l < 2:
                    dve.wait_ge(x_loaded[b * HT + t], 16)
                else:
                    dve.wait_ge(x_added, (l // 2 - 1) * NT + b * HT + t + 1)
                dve.bn_stats(ln_stat[:, b, t, :], x_tok[:, b * HT + t, :]).then_inc(ln_stats, 1)
                dve.wait_ge(ln_stats, HT * l + t + 1)
                dve.bn_aggr(ln_mv[:, b, t, :], ln_stat[:, b, t, :]).then_inc(ln_mean, 1)

            def ln_norm(l, t):
                b = l % 2
                dve.wait_ge(ln_mean, HT * l + t + 1)
                dve.wait_ge(ln_rs, HT * l + t + 1)
                atleast(dve, ln_turned, HT * (l - 1) + t + 1)
                if l == 4:
                    dve.wait_ge(wout_lo_done, 1)
                dve.tensor_scalar(xn[:, t, :], x_tok[:, b * HT + t, :], ln_mv[:, b, t, 0:1],
                                  ln_rstd[:, b, t:t + 1], ALU.subtract, ALU.mult).then_inc(ln_normed, 1)

            def ln_rest(l, t):
                b, n = l % 2, HT * l + t
                cols = slice((b * HT + t) * P, (b * HT + t + 1) * P)
                dve.wait_ge(ln_hi, n + 1)
                dve.tensor_tensor(xnT_lo[:, :, cols], lnT_bank(l, t)[:, :].rearrange("p (a b) -> p a b", b=P),
                                  xnT_hi[:, :, cols].bitcast(F32), ALU.subtract).then_inc(ln_lo, 1)

            def each(f, l):
                for t in range(HT):
                    f(l, t)

            def lo_of(dst, src, hi):
                dve.tensor_tensor(dst, src, hi.bitcast(F32), ALU.subtract).then_inc(w_lo, 1)

            def ffn(n, b):
                r0, k0 = RAW_FFN[n] + b * FT, (2 * n + b) * FT

                def split_gate_up(k, parity):
                    slot, rs = (k0 + parity) % 2, (r0 + parity) % 2
                    wait_raw(dve, r0, k, parity)
                    dve.wait_ge(w_hi, k * 2 + (2 * r0 + 1))
                    atleast(dve, up_done, k + (k0 - 1))
                    lo_of(gu_lo[:, slot, :, :, :].rearrange("p a b c -> p (a b c)"), raw[:, rs, 0:2 * D],
                          gu_hi[:, slot, :, :, :].rearrange("p a b c -> p (a b c)"))

                def split_down(k, parity):
                    slot, rs = (k0 + parity) % 2, (r0 + parity) % 2
                    dve.wait_ge(w_hi, k * 2 + (2 * r0 + 2))
                    wait_down(dve, 2 * n + b, k)
                    lo_of(dn_lo[:, slot, :], raw[:, rs, 2 * D:], dn_hi[:, slot, :])

                def step(k, parity, more=True):
                    if more:
                        split_gate_up(k + 1, 1 - parity)
                    gated(k, parity)
                    if more:
                        split_down(k + 1, 1 - parity)

                def gated(k, parity):
                    slot = (k0 + parity) % 2
                    dve.wait_ge(silu_done, k + (k0 + 1))
                    dve.wait_ge(up_done, k + (k0 + 1))
                    atleast(dve, hid_lo_done, k + (k0 - 1))
                    atleast(dve, hid_hi_done, k + (k0 - 1))
                    dve.tensor_tensor(hid[:, slot, :], up_ps[slot][:, :], silu[:, slot, :],
                                      ALU.mult).then_inc(hid_done, 1)
                    dve.wait_ge(hid_hi_done, k + (k0 + 1))
                    dve.wait_ge(hid_done, k + (k0 + 1))
                    wait_down(dve, 2 * n + b, k)
                    dve.tensor_tensor(hid_lo[:, slot, :], hid[:, slot, :], hid_hi[:, slot, :].bitcast(F32),
                                      ALU.subtract).then_inc(hid_lo_done, 1)

                if b == 0:
                    split_gate_up(0, 0)
                    if n == 0:
                        each(ln_rest, 0)
                    split_down(0, 0)
                else:
                    add_y(n, 0)
                inside = LN_INSIDE.get((n, b))
                split_gate_up(1, 1)
                if inside:
                    each(ln_stat_of, inside)
                gated(0, 0)
                split_down(1, 1)
                if inside:
                    each(ln_norm, inside)
                    each(ln_rest, inside)
                step(1, 1)
                with dve.Fori(0, PAIRS) as i:
                    step(i * 2 + 2, 0)
                    step(i * 2 + 3, 1)
                    if (n, b) == (0, 1):
                        for c, (lo, hi, cols) in enumerate(((wqk_lo, wqk_hi, slice(0, 2 * D)),
                                                            (wv_lo, wv_hi, slice(2 * D, 3 * D)))):
                            dve.wait_ge(wqkv_hi_done, i * 2 + (c + 1))
                            dve.tensor_tensor(lo[:, bass.ds(i, 1), :], raw_qkv[:, bass.ds(i, 1), cols],
                                              hi[:, bass.ds(i, 1), :].bitcast(F32),
                                              ALU.subtract).then_inc(wqkv_lo_done, 1)
                step(FT - 1, 0, more=b == 0)

            def add_y(n, b):
                for t in range(HT):
                    dve.wait_ge(y_done, HT * (2 * n + b) + t + 1)
                    dve.scalar_tensor_tensor(out=x_tok[:, b * HT + t, :], in0=y_ps[t][:, :], scalar=0.5,
                                             in1=x_tok[:, b * HT + t, :], op0=ALU.mult,
                                             op1=ALU.add).then_inc(x_added, 1)

            each(ln_stat_of, 0)
            each(ln_norm, 0)
            ffn(0, 0)
            ffn(0, 1)
            add_y(0, 1)
            each(ln_stat_of, 3)
            each(ln_norm, 3)
            dve.wait_ge(v_ones, 1)

            def qk_clip(t):
                slot = t % 2
                for c in range(2):
                    dve.wait_ge(qk_done, 2 * t + c + 1)
                    atleast(dve, qk_turned, t - 1)
                    dve.tensor_scalar(qk[:, slot, c, :], qk_ps[slot][c][:, :], CLIP, -CLIP, ALU.min,
                                      ALU.max).then_inc(clipped, 1)
                for c in range(2):
                    dve.wait_ge(clipped, 2 * t + c + 1)
                    dve.bn_stats(qk_stat[:, slot, c, :], qk[:, slot, c, :]).then_inc(qk_stats, 1)
                for c in range(2):
                    dve.wait_ge(qk_stats, 2 * t + c + 1)
                    ins = dve.bn_aggr(qk_mv[:, slot, c, :], qk_stat[:, slot, c, :])
                ins.then_inc(qk_mean, 1)

            def qk_norm(t):
                slot = t % 2
                dve.wait_ge(qk_mean, t + 1)
                dve.wait_ge(qk_rs, t + 1)
                for c in range(2):
                    ins = dve.tensor_scalar(qk[:, slot, c, :], qk[:, slot, c, :], qk_mv[:, slot, c, 0:1],
                                            qk_rstd[:, slot, c:c + 1], ALU.subtract, ALU.mult)
                ins.then_inc(qk_normed, 1)

            def rest1(t):
                slot, pair, cols = t % 2, (t // 2) % 2, slice((t % 2) * P, (t % 2 + 1) * P)
                dve.wait_ge(part0_done, t + 1)
                atleast(dve, part2_done, t - 1)
                for c in range(2):
                    ins = dve.tensor_tensor(qkT_rest[:, slot, c, :, :], qkT[:, slot, c, :, :],
                                            parts[:, pair, :, c, 0, cols], ALU.subtract)
                ins.then_inc(rest1_done, 1)

            def rest2(t):
                slot, pair, cols = t % 2, (t // 2) % 2, slice((t % 2) * P, (t % 2 + 1) * P)
                dve.wait_ge(part1_done, t + 1)
                for c in range(2):
                    ins = dve.tensor_tensor(parts[:, pair, :, c, 2, cols], qkT_rest[:, slot, c, :, :],
                                            parts[:, pair, :, c, 1, cols], ALU.subtract)
                ins.then_inc(part2_done, 1)

            def v_clip(t):
                dve.wait_ge(v_done, t + 1)
                dve.tensor_scalar(v_aug[:, t, 0:H * VC].rearrange("p (h c) -> p h c", c=VC)[:, :, 0:HD],
                                  v_ps[t % 2][:, :].rearrange("p (h c) -> p h c", c=HD), CLIP, -CLIP, ALU.min,
                                  ALU.max).then_inc(v_clipped, 1)

            for t in range(NT):
                qk_clip(t)
                if t > 1:
                    rest2(t - 2)
                qk_norm(t)
                if t > 0:
                    rest1(t - 1)
                if t < HT // 2:
                    for c in range(2):
                        ln_rest(3, 2 * t + c)
            rest2(NT - 2)
            v_clip(0)
            rest1(NT - 1)
            v_clip(1)
            rest2(NT - 1)
            for t in range(2, NT):
                v_clip(t)
            dve.wait_ge(wout_hi_done, 1)
            dve.tensor_tensor(wout_lo[:, :, :], xn[:, :, :], wout_hi[:, :, :].bitcast(F32),
                              ALU.subtract).then_inc(wout_lo_done, 1)

            def ring_a_use(s, k, parity, use):
                kind, what = use
                ps = ring_a[(parity + k) % RING]
                dve.wait_ge(ring_a_done, use_base(s) + (k + 1))
                if kind == "max":
                    h, c = what
                    dve.reduce_max(maxp[:, h, c:c + 1], ps[:, 0:MAX_CHUNKS[c][2]], AX_X).then_inc(ring_a_used, 1)
                elif kind == "maxT":
                    atleast(dve, max_out, s * 16)
                    dve.tensor_copy(maxT[:, :], ps[0:PARTS * QH * NT, 0:P // 2].bitcast(BF16)).then_inc(ring_a_used, 1)
                else:
                    store_outputs(s - 1, what, ps)

            def split_max(s):
                n0 = s * 5
                dve.wait_ge(ring_a_used, use_base(s))
                dve.tensor_tensor(maxv[:, :, HT:NT], maxp[:, :, HT:NC:2], maxp[:, :, HT + 1:NC:2],
                                  ALU.max).then_inc(max_step, 1)
                dve.tensor_copy(maxv[:, :, 0:HT], maxp[:, :, 0:HT]).then_inc(max_step, 1)
                dve.wait_ge(max_step, n0 + 2)
                flat = maxv[:, :, :].rearrange("p h t -> p (h t)")
                dve.tensor_scalar(max_parts[:, 0, :], flat, -1.0, None, ALU.mult).then_inc(max_step, 1)
                dve.wait_ge(max_step, n0 + 3)
                dve.scalar_tensor_tensor(out=maxr[:, :], in0=flat, scalar=-1.0, in1=max_parts[:, 0, :], op0=ALU.mult,
                                         op1=ALU.subtract).then_inc(max_step, 1)
                dve.wait_ge(max_step, n0 + 4)
                dve.tensor_copy(max_parts[:, 1, :], maxr[:, :]).then_inc(max_step, 1)
                dve.wait_ge(max_step, n0 + 5)
                dve.tensor_tensor(max_parts[:, 2, :], maxr[:, :], max_parts[:, 1, :],
                                  ALU.subtract).then_inc(max_parts_done, 1)

            def store_outputs(s, b, ps):
                o = ps[:, :].rearrange("p (t h c) -> p t h c", t=HT, c=VW)
                dve.reciprocal(rsum[:, b, :, :], o[:, :, :, HD]).then_inc(rsum_done, 1)
                dve.wait_ge(rsum_done, s * 2 + (b + 1))
                if isinstance(s, int):
                    dst = attn[:, b * HT:(b + 1) * HT, s * QH * HD:(s + 1) * QH * HD]
                else:
                    dst = attn[:, b * HT:(b + 1) * HT, bass.ds(s * (QH * HD), QH * HD)]
                dve.tensor_tensor(dst.rearrange("p t (h c) -> p t h c", c=HD), o[:, :, :, 0:HD],
                                  rsum[:, b, :, :].unsqueeze(3).to_broadcast([P, HT, QH, HD]),
                                  ALU.mult).then_inc(ring_a_used, 1)

            def step(s, parity, kind):
                k = 0
                if 0 <= kind < NQ:
                    split_max(s)
                for place in steps_of(kind):
                    for uses in place:
                        for use in uses:
                            ring_a_use(s, k, parity, use)
                            k += 1

            parity0 = (n_uses(-1) + n_uses(0)) % RING
            step(-1, 0, -1)
            step(0, n_uses(-1) % RING, 0)
            with dve.Fori(0, (NQ - 2) // SLOTS) as i:
                for c in range(SLOTS):
                    step(i * SLOTS + (1 + c), parity0, 1)
            step(NQ - 1, parity0, NQ - 1)
            step(NQ, use_base(NQ) % RING, NQ)

            def attn_rest(t):
                dve.wait_ge(aT_hi_done, t + 1)
                dve.tensor_tensor(aT_lo[:, t % 2, :, :], attnT_ps[t % 2][:, :].rearrange("p (a b) -> p a b", b=P),
                                  aT_hi[:, t % 2, :, :].bitcast(F32), ALU.subtract).then_inc(aT_lo_done, 1)

            attn_rest(0)
            for t in range(NT):
                if t + 1 < NT:
                    attn_rest(t + 1)
                dve.wait_ge(proj_done, t + 1)
                dve.tensor_tensor(x_tok[:, t, :], proj_ps[t % 2][:, :], x_tok[:, t, :], ALU.add).then_inc(x_added, 1)
                if t < HT:
                    ln_stat_of(4, t)
                if 0 < t <= HT:
                    ln_norm(4, t - 1)
                if 0 <= t - LN_BEHIND < HT:
                    ln_rest(4, t - LN_BEHIND)
            ffn(1, 0)
            ffn(1, 1)
            add_y(1, 1)


def _bf16_bits(a):
    return (np.ascontiguousarray(a, np.float32).view(np.uint32) >> 16).astype(np.uint16)


def _bf16_parts(a):
    rest, found = np.asarray(a, np.float32), []
    for _ in range(PARTS):
        part = (rest.view(np.uint32) & np.uint32(0xFFFF0000)).view(np.float32)
        found.append(part)
        rest = rest - part
    return found


def _bias_rows():
    slope = (1.0 / np.power(2.0, np.arange(1, H + 1) * (8 / H))).astype(np.float32)
    pos = np.arange(S)
    low = pos % 8
    high = pos - low
    q = np.zeros((H, N_BIAS, S), np.float32)
    k = np.ones((H, N_BIAS + PARTS, S), np.float32)
    for p, s in enumerate(_bf16_parts(slope)):
        for n, where in enumerate((high, low)):
            row = 4 * p + 2 * n
            q[:, row, :], k[:, row, :] = s[:, None], where
            q[:, row + 1, :], k[:, row + 1, :] = where, -s[:, None]
    return [_bf16_bits(a.reshape(NQ, QH, a.shape[1], S).transpose(0, 2, 1, 3)) for a in (q, k)]


def _constants():
    eye = np.eye(P, dtype=np.float32)
    upper = np.triu(np.ones((P, P), np.float32), 1) * np.float32(MASKED)
    bias_q, bias_k = _bias_rows()
    return {"ident": eye, "ident_b": _bf16_bits(eye), "masks": _bf16_bits(np.stack([upper, upper.T], axis=1)),
            "bias_q": bias_q, "bias_k": bias_k}


def kernel(L0_attn_hidden_states, L0_attn_w_qkv, L0_attn_q_ln_w, L0_attn_q_ln_b, L0_attn_k_ln_w, L0_attn_k_ln_b,
           L0_attn_w_out, L0_ffn_W_gate, L0_ffn_W_up, L0_ffn_W_down):
    import concourse.bacc as _bacc
    from concourse.bass_utils import run_bass_kernel_spmd as _run

    f32 = lambda a: np.asarray(a)
    w_ffn = np.zeros((FT, P, FFN_RAW), np.float32)
    for n, w in enumerate((f32(L0_ffn_W_gate), f32(L0_ffn_W_up))):
        padded = np.zeros((FT * P, D), np.float32)
        padded[0:F] = w
        w_ffn[:, :, n * D:(n + 1) * D] = padded.reshape(FT, P, DT, P).transpose(0, 3, 2, 1).reshape(FT, P, D)
    padded = np.zeros((FT * P, D), np.float32)
    padded[0:F] = f32(L0_ffn_W_down).T
    w_ffn[:, :, 2 * D:] = padded.reshape(FT, P, D)
    by_feature = np.arange(D).reshape(DT, P // HD, HD).transpose(0, 2, 1).ravel()
    order = np.concatenate([by_feature, D + by_feature, 2 * D + np.arange(D)])
    w_qkv = np.ascontiguousarray(f32(L0_attn_w_qkv)[order].T.reshape(DT, P, 3 * D).transpose(1, 0, 2))
    w_out = f32(L0_attn_w_out).T.reshape(DT, P, D).transpose(1, 0, 2)
    column = lambda a, b: np.stack([f32(a)[by_feature].reshape(DT, P).T,
                                   f32(b)[by_feature].reshape(DT, P).T], axis=1)
    arrays = {
        "x": f32(L0_attn_hidden_states).reshape(S, D),
        "w_ffn": w_ffn,
        "w_qkv": w_qkv,
        "w_out": w_out,
        "ln_w": column(L0_attn_q_ln_w, L0_attn_k_ln_w),
        "ln_b": column(L0_attn_q_ln_b, L0_attn_k_ln_b),
        **_constants(),
    }
    nc = _bacc.Bacc("TRN2", target_bir_lowering=False, num_devices=1)
    args = []
    for name, a in arrays.items():
        arrays[name] = np.ascontiguousarray(a)
        ap = nc.dram_tensor(name, a.shape, mybir.dt.from_np(a.dtype), kind="ExternalInput").ap()
        args.append(ap.bitcast(BF16) if a.dtype == np.uint16 else ap)
    out = nc.dram_tensor("y", (S, D), F32, kind="ExternalOutput").ap()
    x, w_f, w_q, w_o, l_w, l_b, ident, ident_b, masks, bias_q, bias_k = args
    macaron_block(nc, x, w_f, w_q, w_o, l_w, l_b, ident, ident_b, masks, bias_q, bias_k, out)
    r = _run(nc, [arrays], core_ids=[0])
    return r.results[0]["y"].reshape(1, S, D)
```

```python
from contextlib import ExitStack

import numpy as np

import concourse.bass as bass
from concourse import mybir

F32 = mybir.dt.float32
F32R = mybir.dt.float32r
BF16 = mybir.dt.bfloat16
ALU = mybir.AluOpType
ACT = mybir.ActivationFunctionType
AX_X = mybir.AxisListType.X

P = 128
S = 1024
D = 512
F = 1376
H = 32
HD = D // H
NT = S // P
DT = D // P
HALF = S // 2
HT = NT // 2
FT = -(-F // P)
QH = 4
NQ = H // QH
PARTS = 3
CLIP = 8.0
EPS = 1e-5
SCALE = HD ** -0.5
MASKED = -1e30

Q_RUNS = ((0, 3), (0, 2), (0, 1))
K_RUNS = ((0, 1), (0, 1), (0, 1), (1, 1), (1, 1), (2, 1))
N_PAIRS = 6
ROW_BIAS = N_PAIRS * HD
N_BIAS = 4 * PARTS
ROW_MAX = ROW_BIAS + N_BIAS
N_ROWS = ROW_MAX + PARTS
VC = HD + 1
VW = 32
SLOTS = 3
RING = 3

FFN_RAW = 3 * D

RAW_FFN = (0, 2 * FT)
PAIRS = (FT - 3) // 2
assert PAIRS == DT

LN_INSIDE = {(0, 0): 1, (0, 1): 2, (1, 0): 5}

MAX_CHUNKS = []
for _t in range(NT):
    for _j in range(_t // HT + 1):
        _diag = _t // HT == _j
        MAX_CHUNKS.append((_t, _j, (_t % HT + 1) * P if _diag else HALF, (_t % HT) * P if _diag else None))
KEY_GROUPS = [(b, kt, max(b * HALF, kt * P), kt // HT == b) for b in range(2) for kt in range((b + 1) * HT)]
NC = len(MAX_CHUNKS)
NG = len(KEY_GROUPS)
HALF_END = (HT - 1, NG - 1)


LAG = 6


def groups_of(s):
    return [p - LAG for p in range(NG) if (s > 0 or p >= LAG) and (s < NQ or p < LAG)]


def steps_of(s):
    uses = [[[] for _ in range(QH)] for _ in range(NG)]
    width = [(b + 1) * HALF - q0 for b, kt, q0, diag in KEY_GROUPS]
    work = [3 + (2 * width[p - LAG] + 3 * width[p - LAG - 1]) / HALF / 5 for p in range(NG)]
    if s < NQ - 1:
        chunks = [("max", (h, c)) for h in range(QH) for c in range(NC)]
        if s < 0:
            chunks.sort(key=lambda use: (use[1][1] >= HT) + MAX_CHUNKS[use[1][1]][1])
        elif s == 0:
            uses[0][0] += chunks[:WHILE_MOVED]
            chunks = chunks[WHILE_MOVED:]
        first = LAG if s == 0 else 0
        total, count, given = sum(work[first:]), len(chunks), 0
        for p in range(first, NG):
            for h in range(QH):
                due = round(count * (sum(work[first:p]) + work[p] * (h + 1) / QH) / total)
                uses[p][h] += chunks[given:due]
                given = due
    if 0 <= s < NQ:
        p = 0 if s == 0 else MAX_PLACE
        uses[p][0].insert(MAX_BEHIND if s == 0 else 0, ("maxT", None))
    if s > 0:
        uses[OUT_PLACE[0]][1].append(("out", 0))
        uses[OUT_PLACE[1]][0].append(("out", 1))
    return uses


OUT_PLACE = {1: LAG + 2, 0: (LAG + HT + 2) % NG}
MAX_PLACE = 1
EARLY = QH * HT
EARLY_QUERIES = EARLY + QH * (NT - HT)
EARLY_FROM = 4
WHILE_MOVED = 12
MAX_BEHIND = 3


def n_uses(s):
    return sum(len(uses) for place in steps_of(s) for uses in place)


def use_base(s):
    first = n_uses(-1)
    if isinstance(s, int) and s < 0:
        return 0
    if isinstance(s, int) and s == 0:
        return first
    if isinstance(s, int) and s == NQ:
        return use_base(NQ - 1) + n_uses(NQ - 1)
    return (s - 1) * n_uses(1) + (first + n_uses(0))


def macaron_block(nc, x_in, w_ffn, w_qkv, w_out, ln_w, ln_b, ident_in, ident_b_in, mask_in, masks_in,
                  bias_q, bias_k, out):
    ctx = ExitStack()
    with ctx:
        at = [-(-nc.sbuf_base // 64) * 64]

        def place(name, shape, dt, offset=None):
            size = int(np.prod(shape[1:])) * (2 if dt == BF16 else 4)
            if offset is None:
                offset, at[0] = at[0], -(-(at[0] + size) // 64) * 64
            return nc.alloc_sbuf_tensor_at(name, shape, dt, offset=offset)

        def region(size):
            start, at[0] = at[0], at[0] + size
            return start

        def sem(name):
            return ctx.enter_context(nc.semaphore(name))

        KB = 1024
        x_tok = place("x_tok", [P, NT, D], F32)
        xnT_at = region(32 * KB)
        xnT_hi = place("xnT_hi", [P, DT, S], F32R, xnT_at)
        xnT_lo = place("xnT_lo", [P, DT, S], F32R, xnT_at + 16 * KB)
        raw = place("raw", [P, 2, FFN_RAW], F32)
        xn = place("xn", [P, HT, D], F32)
        v_aug = place("v_aug", [P, NT, H * VC + HD], F32)
        ident = place("ident", [P, P], F32)
        ident_b = place("ident_b", [P, P], BF16)
        mask = place("mask", [P, P], BF16)
        masks = place("masks", [P, HALF], F32)
        masked = place("masked", [P, RING, HALF], F32)
        lnw = place("lnw", [P, 2, DT], F32)
        lnb = place("lnb", [P, 2, DT], F32)
        ln_stat = place("ln_stat", [P, 2, HT, 6], F32)
        ln_mv = place("ln_mv", [P, 2, HT, 2], F32)
        ln_var = place("ln_var", [P, 2, HT], F32)
        ln_rstd = place("ln_rstd", [P, 2, HT], F32)
        minus_half = place("minus_half", [P, HT], F32)
        maxp = place("maxp", [P, QH, NC], F32)
        qk_stat = place("qk_stat", [P, 2, 2, 6], F32)
        qk_mv = place("qk_mv", [P, 2, 2, 2], F32)
        qk_var = place("qk_var", [P, 2, 2], F32)
        qk_rstd = place("qk_rstd", [P, 2, 2], F32)
        A = region(40 * KB)
        gu_hi = place("gu_hi", [P, 2, 2, DT, P], F32R, A)
        gu_lo = place("gu_lo", [P, 2, 2, DT, P], F32R, A + 8 * KB)
        dn_hi = place("dn_hi", [P, 2, D], F32R, A + 16 * KB)
        dn_lo = place("dn_lo", [P, 2, D], F32R, A + 20 * KB)
        silu = place("silu", [P, 2, HALF], F32, A + 24 * KB)
        hid = place("hid", [P, 2, HALF], F32, A + 28 * KB)
        hid_hi = place("hid_hi", [P, 2, HALF], F32R, A + 32 * KB)
        hid_lo = place("hid_lo", [P, 2, HALF], F32R, A + 36 * KB)
        parts = place("parts", [P, 2, DT, 2, PARTS, 2 * P], BF16, A)
        attn = place("attn", [P, NT, D], F32, A)
        oT = place("oT", [P, 2, HALF], F32, A + 16 * KB)
        maxv = place("maxv", [P, QH, NT], F32, A + 20 * KB + 512)
        maxr = place("maxr", [P, QH * NT], F32, A + 21 * KB)
        max_parts = place("max_parts", [P, PARTS, QH * NT], BF16, A + 21 * KB + 512)
        maxT = place("maxT", [PARTS * QH * NT, P], BF16, A + 22 * KB)
        rsum = place("rsum", [P, 2, HT, QH], F32, A + 23 * KB)
        wout_hi = place("wout_hi", [P, DT, D], F32R, A + 24 * KB)
        wout_lo = place("wout_lo", [P, DT, D], F32R, A + 32 * KB)
        B = region(72 * KB)
        wqk_hi = place("wqk_hi", [P, DT, 2 * D], F32R, B)
        wqk_lo = place("wqk_lo", [P, DT, 2 * D], F32R, B + 16 * KB)
        wv_hi = place("wv_hi", [P, DT, D], F32R, B + 32 * KB)
        wv_lo = place("wv_lo", [P, DT, D], F32R, B + 40 * KB)
        raw_qkv = place("raw_qkv", [P, DT, 3 * D], F32, B + 48 * KB)
        qk = place("qk", [P, 2, 2, D], F32, B + 48 * KB)
        qkT = place("qkT", [P, 2, 2, DT, P], F32, B + 56 * KB)
        qkT_rest = place("qkT_rest", [P, 2, 2, DT, P], F32, B + 64 * KB)
        rows = place("rows", [P, SLOTS, 2, QH, S], BF16, B)
        q_rows, k_rows = rows[:, :, 0], rows[:, :, 1]
        probs = place("probs", [P, 3, QH, HALF], F32, B + 48 * KB)
        v_quad = place("v_quad", [P, SLOTS, NT, QH * VC + HD], F32, xnT_at)
        aT_hi = place("aT_hi", [P, 2, DT, P], F32R, B)
        aT_lo = place("aT_lo", [P, 2, DT, P], F32R, B + 4 * KB)

        bank = [ctx.enter_context(nc.psum_tensor(f"bank{i}", [P, 512], F32)) for i in range(8)]
        gate_ps, up_ps, y_ps = bank[0:2], bank[2:4], bank[4:8]
        lnT_ps = {0: bank[0:4], 3: bank[4:6]}
        for l in LN_INSIDE.values():
            lnT_ps[l] = y_ps
        qk_ps, qkT_ps = [bank[0:2], bank[2:4]], bank[6:8]
        v_ps = bank[4:6] + bank[3:4]
        ring_a, ring_b, o_ps = bank[0:3], bank[3:6], bank[6:8]
        wide_b, last_a = ring_b + ring_a[0:2], ring_a[2]
        proj_ps, attnT_ps = bank[4:6], [bank[6], bank[0]]
        lnT_ps[4] = [bank[i] for i in (1, 2, 3, 7)]

        qk_scr = nc.dram_tensor("qk_scr", (DT, 2, PARTS, P, S), BF16, kind="Internal").ap()
        max_scr = nc.dram_tensor("max_scr", (2, PARTS, QH * S), BF16, kind="Internal").ap()

        ident_loaded = sem("ident_loaded")
        const_in = sem("const_in")
        x_loaded = [sem(f"x_loaded{i}") for i in range(NT)]
        raw_in = [sem(f"raw_in{i}") for i in range(2)]
        raw_qkv_in = sem("raw_qkv_in")
        raw_out_in = sem("raw_out_in")
        w_hi = sem("w_hi")
        w_lo = sem("w_lo")
        wqkv_hi_done = sem("wqkv_hi_done")
        wqkv_lo_done = sem("wqkv_lo_done")
        wout_hi_done = sem("wout_hi_done")
        wout_lo_done = sem("wout_lo_done")
        half_set = sem("half_set")
        q_scaled = sem("q_scaled")
        v_ones = sem("v_ones")
        ln_stats = sem("ln_stats")
        ln_mean = sem("ln_mean")
        ln_eps = sem("ln_eps")
        ln_rs = sem("ln_rs")
        ln_normed = sem("ln_normed")
        ln_turned = sem("ln_turned")
        ln_hi = sem("ln_hi")
        ln_lo = sem("ln_lo")
        gate_done = sem("gate_done")
        up_done = sem("up_done")
        down_done = sem("down_done")
        y_done = sem("y_done")
        silu_done = sem("silu_done")
        hid_done = sem("hid_done")
        hid_hi_done = sem("hid_hi_done")
        hid_lo_done = sem("hid_lo_done")
        x_added = sem("x_added")
        qk_done = sem("qk_done")
        v_done = sem("v_done")
        clipped = sem("clipped")
        v_clipped = sem("v_clipped")
        qk_stats = sem("qk_stats")
        qk_mean = sem("qk_mean")
        qk_eps = sem("qk_eps")
        qk_rs = sem("qk_rs")
        qk_normed = sem("qk_normed")
        qk_turned = sem("qk_turned")
        qkT_done = sem("qkT_done")
        part0_done = sem("part0_done")
        rest1_done = sem("rest1_done")
        part1_done = sem("part1_done")
        part2_done = sem("part2_done")
        parts_out = [sem(f"parts_out{i}") for i in range(2)]
        rows_early = sem("rows_early")
        rows_queries = sem("rows_queries")
        rows_in = [sem(f"rows_in{i}") for i in range(SLOTS)]
        v_in = [sem(f"v_in{i}") for i in range(SLOTS)]
        max_out = sem("max_out")
        max_in = [sem(f"max_in{i}") for i in range(SLOTS)]
        ring_a_done = sem("ring_a_done")
        ring_a_used = sem("ring_a_used")
        chunk_seen = sem("chunk_seen")
        ring_b_done = sem("ring_b_done")
        probs_done = sem("probs_done")
        pv_done = sem("pv_done")
        oT_done = sem("oT_done")
        max_step = sem("max_step")
        max_parts_done = sem("max_parts_done")
        rsum_done = sem("rsum_done")
        attn_turned = sem("attn_turned")
        aT_hi_done = sem("aT_hi_done")
        aT_lo_done = sem("aT_lo_done")
        proj_done = sem("proj_done")
        out_sent = sem("out_sent")

        def atleast(eng, s, value):
            if not isinstance(value, int) or value > 0:
                eng.wait_ge(s, value)

        def wait_down(eng, half, k):
            if not isinstance(k, int) or k >= 2:
                eng.wait_ge(down_done, k + ((FT - 1) * half - 1))
            elif half and k == 0:
                eng.wait_ge(down_done, (FT - 1) * half)
            elif half:
                eng.wait_ge(y_done, HT * half)

        def wait_raw(eng, r0, k, parity):
            eng.wait_ge(raw_in[(r0 + parity) % 2], (k + (r0 - (r0 + parity) % 2 + 2)) * 8)

        def bank_a(s, parity, k):
            if isinstance(s, int) and s >= NQ - 1:
                return last_a, 1
            return ring_a[(parity + k) % RING], RING

        def bank_b(s, u, h):
            m, last = QH * (u + LAG) + h, QH * NG
            if isinstance(s, int) and s == NQ - 1:
                return wide_b[m % len(wide_b)], RING if m < RING else None if m < len(wide_b) else len(wide_b)
            ago = RING
            if isinstance(s, int) and s == NQ and m < RING:
                ago = m + 1 + (last - 1 - m % RING) % len(wide_b)
            return ring_b[m % RING], ago

        def lnT_bank(l, t):
            return lnT_ps[l][t % len(lnT_ps[l])]

        last_use = use_base(NQ) + n_uses(NQ)

        def use_of(s, use):
            k = 0
            for place in steps_of(s if isinstance(s, int) else 1):
                for uses in place:
                    for this in uses:
                        k += 1
                        if this == use:
                            return use_base(s) + k
            raise ValueError(use)

        constants = ((ident_b, ident_b_in), (mask, mask_in), (masks, masks_in), (lnw, ln_w), (lnb, ln_b))
        V_LEAD = len(v_ps)
        n_rows_dma = len(Q_RUNS) + len(K_RUNS) + 2
        early = [use for place in steps_of(-1) for uses in place for use in uses][:EARLY]

        def early_uses(t, dt):
            n, places = max((t - EARLY_FROM) * DT + dt, 0), (NT - EARLY_FROM) * DT
            return EARLY * n // places, EARLY * (n + 1) // places if t >= EARLY_FROM else 0

        LN_BEHIND = NT - 1 - HT
        block = ctx.enter_context(nc.Block())

        @block.sync
        def _(sp):
            def load_x(t):
                sp.dma_start(x_tok[:, t, :], x_in[t * P:(t + 1) * P, :]).then_inc(x_loaded[t], 16)

            def load_raw(r, parity, src, width):
                atleast(sp, w_hi, 2 * r - 2)
                atleast(sp, w_lo, 2 * r - 2)
                sp.dma_start(raw[:, parity, 0:width], src).then_inc(raw_in[parity], 16)

            def load_first(n):
                load_raw(RAW_FFN[n], RAW_FFN[n] % 2, w_ffn[0], FFN_RAW)

            def load_ffn(n):
                for b in range(2):
                    r0 = RAW_FFN[n] + b * FT
                    if b:
                        load_raw(r0, r0 % 2, w_ffn[0], FFN_RAW)
                    with sp.Fori(0, (FT - 1) // 2) as i:
                        for c in range(2):
                            load_raw(i * 2 + (r0 + 1 + c), (r0 + 1 + c) % 2, w_ffn[i * 2 + (1 + c)], FFN_RAW)
                    if n == 0 and b == 0:
                        sp.dma_start(raw_qkv[:, :, :], w_qkv).then_inc(raw_qkv_in, 16)

            for t in range(HT):
                load_x(t)
            sp.dma_start(ident[:, :], ident_in).then_inc(ident_loaded, 16)
            load_first(0)
            for t in range(HT, NT):
                load_x(t)
            for dst, src in constants:
                sp.dma_start(dst[tuple(slice(None) for _ in src.shape)], src).then_inc(const_in, 16)
            load_ffn(0)
            load_first(1)
            sp.wait_ge(ln_turned, HT * 4)
            sp.dma_start(xn[:, :, :], w_out).then_inc(raw_out_in, 16)

            def load_rows(g, tok=slice(0, S), landed=None, sides=(0, 1)):
                landed = landed or rows_in[g % SLOTS]
                slot, n, heads = g % SLOTS, g * QH * HD // P, slice(g * QH % (P // HD), g * QH % (P // HD) + QH)
                for c in sides:
                    row = 0
                    for part, length in (Q_RUNS, K_RUNS)[c]:
                        src = qk_scr[n, c, part:part + length].rearrange("p (d h) t -> (p d) h t", d=HD)[:, heads, tok]
                        sp.dma_start(rows[row:row + length * HD, slot, c, :, tok], src).then_inc(landed, 16)
                        row += length * HD
                    bias, end = ((bias_q, ROW_MAX), (bias_k, N_ROWS))[c]
                    sp.dma_start(rows[ROW_BIAS:end, slot, c, :, tok], bias[g][:, :, tok]).then_inc(landed, 16)

            for j in range(NT // 2):
                if j >= 2:
                    sp.wait_ge(parts_out[j % 2], 16)
                if j == 2:
                    sp.wait_ge(parts_out[1], 16)
                    sp.wait_ge(qk_done, 2 * NT)
                    load_rows(0, slice(0, HALF), rows_early)
                sp.wait_ge(part2_done, 2 * j + 2)
                sp.dma_start(qk_scr.rearrange("n c p r t -> r (n c p) t")[:, :, j * 2 * P:(j + 1) * 2 * P],
                             parts[:, j % 2].rearrange("r n c p t -> r (n c p) t")).then_inc(parts_out[j % 2], 16)
            for j in range(2):
                sp.wait_ge(parts_out[j], 16 * NT // 4)

            def load_v(g):
                sp.dma_start(v_quad[:, g % SLOTS, :, :],
                             v_aug[:, :, g * QH * VC:(g + 1) * QH * VC + HD]).then_inc(v_in[g % SLOTS], 16)

            def move_max(g):
                sp.wait_ge(ring_a_used, use_of(g, ("maxT", None)))
                if g >= 2:
                    sp.wait_ge(max_in[(g - 2) % SLOTS], 16 * ((g - 2) // SLOTS + 1))
                sp.dma_start(max_scr[g % 2].rearrange("p (r c) -> (p r) c", c=P), maxT[:, :]).then_inc(max_out, 16)
                sp.wait_ge(max_out, 16 * (g + 1))
                sp.dma_start(q_rows[ROW_MAX:N_ROWS, g % SLOTS, :, :],
                             max_scr[g % 2].rearrange("p (h t) -> p h t", h=QH)).then_inc(max_in[g % SLOTS], 16)

            load_rows(0, slice(HALF, S), rows_queries, sides=(0,))
            load_rows(0, slice(HALF, S), sides=(1,))
            load_rows(1)
            sp.wait_ge(v_clipped, NT)
            for g in range(SLOTS - 1):
                load_v(g)
            for s in range(NQ):
                move_max(s)
                if s + 2 < NQ:
                    if s > 0:
                        sp.wait_ge(pv_done, NG * s)
                    load_rows(s + 2)
                    load_v(s + 2)

            load_ffn(1)
            for t in range(NT):
                sp.wait_ge(x_added, 2 * NT + t + 1)
                sp.dma_start(out[t * P:(t + 1) * P, :], x_tok[:, t, :]).then_inc(out_sent, 16)
            sp.wait_ge(out_sent, 16 * NT)

        @block.gpsimd
        def _(pool):
            pool.memset(minus_half[:, :], -0.5).then_inc(half_set, 1)
            pool.wait_ge(half_set, 1)

            def rsqrt(mv_ready, count, mv, var, rstd, eps_sem, rs_sem, done):
                pool.wait_ge(mv_ready, count)
                pool.tensor_scalar(var, mv, EPS, None, ALU.add).then_inc(eps_sem, 1)
                pool.wait_ge(eps_sem, done)
                pool.tensor_tensor(rstd, var, minus_half[:, 0:var.shape[1]], ALU.pow).then_inc(rs_sem, 1)

            def ln(l):
                b = l % 2
                for t in range(HT):
                    n = HT * l + t + 1
                    rsqrt(ln_mean, n, ln_mv[:, b, t, 1:2], ln_var[:, b, t:t + 1], ln_rstd[:, b, t:t + 1],
                          ln_eps, ln_rs, n)

            ln(0)
            pool.wait_ge(const_in, 16 * len(constants))
            for a in (lnw, lnb):
                pool.tensor_scalar(a[:, 0, :], a[:, 0, :], SCALE, None, ALU.mult).then_inc(q_scaled, 1)
            pool.memset(v_aug[:, :, :], 1.0).then_inc(v_ones, 1)
            for l in range(1, 4):
                ln(l)
            for t in range(NT):
                rsqrt(qk_mean, t + 1, qk_mv[:, t % 2, :, 1], qk_var[:, t % 2, :], qk_rstd[:, t % 2, :],
                      qk_eps, qk_rs, t + 1)
            pool.wait_ge(wout_hi_done, 1)
            pool.tensor_tensor(wout_lo[:, :, :], xn[:, :, :], wout_hi[:, :, :].bitcast(F32),
                               ALU.subtract).then_inc(wout_lo_done, 1)
            for l in range(4, 6):
                ln(l)

        @block.tensor
        def _(pe):
            def three_pass(dst, a_hi, a_lo, b_hi, b_lo, start, stop):
                pe.matmul(dst, a_hi, b_hi, start=start, stop=False)
                pe.matmul(dst, a_hi, b_lo, start=False, stop=False)
                return pe.matmul(dst, a_lo, b_hi, start=False, stop=stop)

            def ln_turn(l, t):
                n, ps = HT * l + t, lnT_bank(l, t)
                pe.wait_ge(ln_normed, n + 1)
                if t >= len(lnT_ps[l]):
                    pe.wait_ge(ln_lo, n + 1 - len(lnT_ps[l]))
                for dt in range(DT):
                    ins = pe.transpose(ps[:, dt * P:(dt + 1) * P], xn[:, t, dt * P:(dt + 1) * P], ident[:, :])
                ins.then_inc(ln_turned, 1)

            def ffn(n, b):
                r0, k0, inside = RAW_FFN[n] + b * FT, (2 * n + b) * FT, LN_INSIDE.get((n, b))
                tok = slice(b * HALF, (b + 1) * HALF)

                def gate_up(k, parity):
                    slot = (k0 + parity) % 2
                    pe.wait_ge(w_hi, k * 2 + (2 * r0 + 1))
                    pe.wait_ge(w_lo, k * 2 + (2 * r0 + 1))
                    for which, ps, freed, done in ((0, gate_ps, silu_done, gate_done), (1, up_ps, hid_done, up_done)):
                        atleast(pe, freed, k + (k0 - 1))
                        for dt in range(DT):
                            ins = three_pass(ps[slot][:, :], gu_hi[:, slot, which, dt, :], gu_lo[:, slot, which, dt, :],
                                             xnT_hi[:, dt, tok], xnT_lo[:, dt, tok], dt == 0, dt == DT - 1)
                        ins.then_inc(done, 1)

                def down(k, parity, first=False, last=False):
                    slot = (k0 + parity) % 2
                    pe.wait_ge(w_hi, k * 2 + (2 * r0 + 2))
                    pe.wait_ge(w_lo, k * 2 + (2 * r0 + 2))
                    pe.wait_ge(hid_lo_done, k + (k0 + 1))
                    for t in range(HT):
                        if first and inside:
                            pe.wait_ge(ln_lo, HT * inside + t + 1)
                        elif first:
                            pe.wait_ge(x_added, NT * (2 * n) + t + 1)
                        cols = slice(t * P, (t + 1) * P)
                        ins = three_pass(y_ps[t][:, :], hid_hi[:, slot, cols], hid_lo[:, slot, cols],
                                         dn_hi[:, slot, :], dn_lo[:, slot, :], first, last)
                        if last:
                            ins.then_inc(y_done, 1)
                    if not last:
                        ins.then_inc(down_done, 1)

                pe.wait_ge(ln_lo, HT * (4 * n + b + 1))
                gate_up(0, 0)
                gate_up(1, 1)
                if inside:
                    for t in range(HT):
                        ln_turn(inside, t)
                down(0, 0, first=True)
                with pe.Fori(0, PAIRS) as i:
                    gate_up(i * 2 + 2, 0)
                    down(i * 2 + 1, 1)
                    gate_up(i * 2 + 3, 1)
                    down(i * 2 + 2, 0)
                gate_up(FT - 1, 0)
                down(FT - 2, 1)
                down(FT - 1, 0, last=True)

            pe.wait_ge(ident_loaded, 16)
            for t in range(HT):
                ln_turn(0, t)
            ffn(0, 0)
            ffn(0, 1)

            def project_qk(t):
                if t == 0:
                    pe.wait_ge(wqkv_hi_done, 2 * DT)
                    pe.wait_ge(wqkv_lo_done, 2 * DT)
                if t < HT:
                    pe.wait_ge(ln_lo, HT * 3)
                else:
                    pe.wait_ge(ln_lo, HT * 3 + t - HT + 1)
                cols = slice(t * P, (t + 1) * P)
                for c in range(2):
                    atleast(pe, clipped, 2 * (t - 2) + c + 1)
                    for dt in range(DT):
                        w = slice(c * D, (c + 1) * D)
                        ins = three_pass(qk_ps[t % 2][c][:, :], xnT_hi[:, dt, cols], xnT_lo[:, dt, cols],
                                         wqk_hi[:, dt, w], wqk_lo[:, dt, w], dt == 0, dt == DT - 1)
                    ins.then_inc(qk_done, 1)

            def project_v(t):
                cols = slice(t * P, (t + 1) * P)
                if t == V_LEAD - 1:
                    pe.wait_ge(clipped, 2 * NT)
                atleast(pe, v_clipped, t - (V_LEAD - 1))
                for dt in range(DT):
                    for k in range(*early_uses(t, dt)):
                        if k == 0:
                            pe.wait_ge(rows_early, 16 * n_rows_dma)
                        ring_a_use(-1, k, 0, early[k], None, 0)
                    ins = three_pass(v_ps[t % V_LEAD][:, :], xnT_hi[:, dt, cols], xnT_lo[:, dt, cols],
                                     wv_hi[:, dt, :], wv_lo[:, dt, :], dt == 0, dt == DT - 1)
                ins.then_inc(v_done, 1)

            def qk_turn(t):
                pe.wait_ge(qk_normed, t + 1)
                atleast(pe, qkT_done, t)
                for c in range(2):
                    for dt in range(DT):
                        ins = pe.transpose(qkT_ps[c][:, dt * P:(dt + 1) * P], qk[:, t % 2, c, dt * P:(dt + 1) * P],
                                           ident[:, :])
                ins.then_inc(qk_turned, 1)

            for t in range(NT):
                project_qk(t)
                if 0 < t <= HT // 2:
                    for c in range(2):
                        ln_turn(3, 2 * (t - 1) + c)
                if t == HT // 2 + 1:
                    pe.wait_ge(const_in, 16 * len(constants))
                if t > 0:
                    qk_turn(t - 1)
            def ring_a_use(s, k, parity, use, slot, next_slot):
                kind, what = use
                ps, ago = bank_a(s, parity, k)
                atleast(pe, ring_a_used, use_base(s) + (k + 1 - ago))
                if kind == "max":
                    h, c = what
                    t, j, width, diag = MAX_CHUNKS[c]
                    ins = pe.matmul(ps[:, 0:width], q_rows[0:ROW_MAX, next_slot, h, t * P:(t + 1) * P],
                                    k_rows[0:ROW_MAX, next_slot, h, j * HALF:j * HALF + width], start=True, stop=True)
                elif kind == "out":
                    b = what
                    pe.wait_ge(oT_done, s * 2 + (b - 1))
                    for t in range(HT):
                        ins = pe.transpose(ps[:, t * P:(t + 1) * P], oT[:, b, t * P:(t + 1) * P], ident[:, :])
                else:
                    pe.wait_ge(max_parts_done, s + 1)
                    ins = pe.transpose(ps[0:PARTS * QH * NT, 0:P // 2].bitcast(BF16),
                                       max_parts[:, :, :].rearrange("p a b -> p (a b)"), ident_b[:, :])
                ins.then_inc(ring_a_done, 1)

            for t in range(NT):
                if t == V_LEAD - 1:
                    qk_turn(NT - 1)
                project_v(t)

            def scores(s, u, h, slot):
                b, kt, q0, diag = KEY_GROUPS[u % NG]
                width = (b + 1) * HALF - q0
                ps, ago = bank_b(s, u, h)
                if ago is None:
                    pe.wait_ge(ring_a_used, use_base(s))
                else:
                    atleast(pe, probs_done, s * (NG * QH) + (QH * u + h + 1 - ago))
                args = (ps[:, 0:width], k_rows[0:N_ROWS, slot, h, kt * P:(kt + 1) * P],
                        q_rows[0:N_ROWS, slot, h, q0:q0 + width])
                ins = pe.matmul(*args, start=True, stop=not diag)
                if diag:
                    ins = pe.matmul(ps[:, 0:P], ident_b[:, :], mask[:, :], start=False, stop=True)
                ins.then_inc(ring_b_done, 1)

            def values(s, u, slot):
                b, kt, q0, diag = KEY_GROUPS[u % NG]
                pe.wait_ge(probs_done, s * (NG * QH) + QH * (u + 1))
                if kt == 0:
                    atleast(pe, oT_done, s * 2 + (b - 1 + 2 * (u // NG)))
                for h in range(QH):
                    ins = pe.matmul(o_ps[b][VW * h:VW * (h + 1), q0 - b * HALF:HALF],
                                    v_quad[:, slot, kt, h * VC:h * VC + VW], probs[:, u % 3, h, 0:(b + 1) * HALF - q0],
                                    start=kt == 0, stop=u % NG in HALF_END)
                ins.then_inc(pv_done, 1)

            def attn_turn(t):
                pe.wait_ge(ring_a_used, use_of(NQ, ("out", t // HT)))
                atleast(pe, aT_lo_done, t - 1)
                for dt in range(DT):
                    ins = pe.transpose(attnT_ps[t % 2][:, dt * P:(dt + 1) * P], attn[:, t, dt * P:(dt + 1) * P],
                                       ident[:, :])
                ins.then_inc(attn_turned, 1)

            def out_project(t):
                if t == 0:
                    pe.wait_ge(wout_hi_done, 1)
                    pe.wait_ge(wout_lo_done, 1)
                pe.wait_ge(aT_lo_done, t + 1)
                atleast(pe, x_added, NT + t - 1)
                for dt in range(DT):
                    ins = three_pass(proj_ps[t % 2][:, :], aT_hi[:, t % 2, dt, :], aT_lo[:, t % 2, dt, :],
                                     wout_hi[:, dt, :], wout_lo[:, dt, :], dt == 0, dt == DT - 1)
                ins.then_inc(proj_done, 1)

            def step(s, slot, parity, kind):
                next_slot = (slot + 1) % SLOTS
                if kind < 0:
                    pe.wait_ge(rows_queries, 16 * (len(Q_RUNS) + 1))
                elif kind < NQ - 1:
                    rows_wait(s, next_slot, kind)
                k = 0
                for p, place in enumerate(steps_of(kind)):
                    u = p - LAG
                    active = kind >= 0 and u in groups_of(kind)
                    behind = kind > 0 and (active or u == 0) or active and u > 0
                    for h in range(QH):
                        for use in place[h]:
                            if kind < 0 and k == EARLY_QUERIES:
                                rows_wait(s, next_slot, kind)
                            if kind >= 0 or k >= EARLY:
                                ring_a_use(s, k, parity, use, slot, next_slot)
                            k += 1
                        if h == QH - 1 and behind:
                            if u == 1 and kind < NQ:
                                v_wait(s, slot)
                            values(s, u - 1, (slot if u > 0 else slot - 1) % SLOTS)
                        if active:
                            if u == 0 and h == 0:
                                max_wait(s, slot)
                            scores(s, u, h, (slot if u >= 0 else slot - 1) % SLOTS)
                    if kind == NQ and u in (-2, -1):
                        attn_turn(u + 2)
                    if kind == NQ and u == 1:
                        out_project(0)


            def rows_wait(s, next_slot, kind):
                others = 16 * (len(Q_RUNS) + 1) if next_slot == 0 else 0
                if isinstance(s, int):
                    pe.wait_ge(rows_in[next_slot], 16 * n_rows_dma * ((s + 1) // SLOTS + 1) - others)
                else:
                    pe.wait_ge(rows_in[next_slot],
                               loop_turn[0] * (16 * n_rows_dma) + (16 * n_rows_dma * loop_turn[1] - others))

            def max_wait(s, slot):
                if isinstance(s, int):
                    pe.wait_ge(max_in[slot], 16 * (s // SLOTS + 1))
                else:
                    pe.wait_ge(max_in[slot], loop_turn[0] * 16 + 16 * loop_turn[2])

            def v_wait(s, slot):
                if isinstance(s, int):
                    pe.wait_ge(v_in[slot], 16 * (s // SLOTS + 1))
                else:
                    pe.wait_ge(v_in[slot], loop_turn[0] * 16 + 16 * loop_turn[2])

            loop_turn = [None, 0, 0]
            parity0 = (n_uses(-1) + n_uses(0)) % RING
            assert n_uses(1) % RING == 0
            step(-1, SLOTS - 1, 0, -1)
            step(0, 0, n_uses(-1) % RING, 0)
            with pe.Fori(0, (NQ - 2) // SLOTS) as i:
                for c in range(SLOTS):
                    loop_turn[:] = [i, (2 + c) // SLOTS + 1, (1 + c) // SLOTS + 1]
                    step(i * SLOTS + (1 + c), (1 + c) % SLOTS, parity0, 1)
            step(NQ - 1, (NQ - 1) % SLOTS, parity0, NQ - 1)
            step(NQ, NQ % SLOTS, use_base(NQ) % RING, NQ)

            for t in range(1, NT):
                if t + 1 < NT:
                    attn_turn(t + 1)
                out_project(t)
                if 0 <= t - LN_BEHIND < HT:
                    ln_turn(4, t - LN_BEHIND)
            ffn(1, 0)
            ffn(1, 1)

        @block.scalar
        def _(act):
            def ln_round(l, t):
                b, n = l % 2, HT * l + t
                cols = slice((b * HT + t) * P, (b * HT + t + 1) * P)
                act.wait_ge(ln_turned, n + 1)
                act.activation(xnT_hi[:, :, cols], lnT_bank(l, t)[:, :].rearrange("p (a b) -> p a b", b=P),
                               ACT.Copy).then_inc(ln_hi, 1)

            def hi_of(dst, src):
                act.activation(dst, src, ACT.Copy).then_inc(w_hi, 1)

            def ffn(n, b):
                r0, k0 = RAW_FFN[n] + b * FT, (2 * n + b) * FT

                def round_gate_up(k, parity):
                    slot, rs = (k0 + parity) % 2, (r0 + parity) % 2
                    wait_raw(act, r0, k, parity)
                    atleast(act, up_done, k + (k0 - 1))
                    hi_of(gu_hi[:, slot, :, :, :].rearrange("p a b c -> p (a b c)"), raw[:, rs, 0:2 * D])

                def round_down(k, parity):
                    slot, rs = (k0 + parity) % 2, (r0 + parity) % 2
                    wait_down(act, 2 * n + b, k)
                    hi_of(dn_hi[:, slot, :], raw[:, rs, 2 * D:])

                def step(k, parity, more=True):
                    slot = (k0 + parity) % 2
                    if more:
                        round_gate_up(k + 1, 1 - parity)
                    act.wait_ge(gate_done, k + (k0 + 1))
                    atleast(act, hid_done, k + (k0 - 1))
                    act.activation(silu[:, slot, :], gate_ps[slot][:, :], ACT.Silu).then_inc(silu_done, 1)
                    act.wait_ge(hid_done, k + (k0 + 1))
                    wait_down(act, 2 * n + b, k)
                    act.activation(hid_hi[:, slot, :], hid[:, slot, :], ACT.Copy).then_inc(hid_hi_done, 1)
                    if more:
                        round_down(k + 1, 1 - parity)

                if b == 0:
                    round_gate_up(0, 0)
                    if n == 0:
                        for t in range(HT):
                            ln_round(0, t)
                    else:
                        ln_round(4, HT - 1)
                    round_down(0, 0)
                step(0, 0)
                if (n, b) in LN_INSIDE:
                    for t in range(HT):
                        ln_round(LN_INSIDE[n, b], t)
                step(1, 1)
                with act.Fori(0, PAIRS) as i:
                    step(i * 2 + 2, 0)
                    step(i * 2 + 3, 1)
                    if (n, b) == (0, 1):
                        act.wait_ge(raw_qkv_in, 16)
                        for dst, cols in ((wqk_hi, slice(0, 2 * D)), (wv_hi, slice(2 * D, 3 * D))):
                            act.activation(dst[:, bass.ds(i, 1), :], raw_qkv[:, bass.ds(i, 1), cols],
                                           ACT.Copy).then_inc(wqkv_hi_done, 1)
                step(FT - 1, 0, more=b == 0)

            ffn(0, 0)
            ffn(0, 1)
            act.wait_ge(q_scaled, 2)

            def second_part(t):
                slot, pair, cols = t % 2, (t // 2) % 2, slice((t % 2) * P, (t % 2 + 1) * P)
                act.wait_ge(rest1_done, t + 1)
                for c in range(2):
                    ins = act.activation(parts[:, pair, :, c, 1, cols], qkT_rest[:, slot, c, :, :], ACT.Copy)
                ins.then_inc(part1_done, 1)

            for t in range(NT):
                slot, pair, cols = t % 2, (t // 2) % 2, slice((t % 2) * P, (t % 2 + 1) * P)
                if t < HT // 2:
                    for c in range(2):
                        ln_round(3, 2 * t + c)
                act.wait_ge(qk_turned, t + 1)
                atleast(act, rest1_done, t - 1)
                for c in range(2):
                    for dt in range(DT):
                        ins = act.activation(qkT[:, slot, c, dt, :], qkT_ps[c][:, dt * P:(dt + 1) * P], ACT.Identity,
                                             bias=lnb[:, c, dt:dt + 1], scale=lnw[:, c, dt:dt + 1])
                ins.then_inc(qkT_done, 1)
                act.wait_ge(qkT_done, t + 1)
                if t % 2 == 0 and t >= 4:
                    act.wait_ge(parts_out[pair], 16)
                for c in range(2):
                    ins = act.activation(parts[:, pair, :, c, 0, cols], qkT[:, slot, c, :, :], ACT.Copy)
                ins.then_inc(part0_done, 1)
                if t > 0:
                    second_part(t - 1)
            second_part(NT - 1)

            act.wait_ge(raw_out_in, 16)
            act.activation(wout_hi[:, :, :], xn[:, :, :], ACT.Copy).then_inc(wout_hi_done, 1)

            def read_outputs(s, b):
                act.wait_ge(pv_done, s * NG + (HALF_END[b] + 1))
                if not (isinstance(s, int) and s == 0):
                    act.wait_ge(ring_a_done, use_of(s, ("out", b)))
                act.activation(oT[:, b, :], o_ps[b][:, :], ACT.Copy).then_inc(oT_done, 1)

            def attn_round(t):
                act.wait_ge(attn_turned, t + 1)
                atleast(act, proj_done, t - 1)
                act.activation(aT_hi[:, t % 2, :, :], attnT_ps[t % 2][:, :].rearrange("p (a b) -> p a b", b=P),
                               ACT.Copy).then_inc(aT_hi_done, 1)

            def step(s, kind):
                for u in groups_of(kind):
                    b, kt, q0, diag = KEY_GROUPS[u % NG]
                    width = (b + 1) * HALF - q0
                    atleast(act, pv_done, s * NG + (u - 2))
                    for h in range(QH):
                        act.wait_ge(ring_b_done, s * (NG * QH) + (QH * u + h + 1))
                        act.activation(probs[:, u % 3, h, 0:width], bank_b(s, u, h)[0][:, 0:width],
                                       ACT.Exp).then_inc(probs_done, 1)
                    if u == 0 and kind > 0:
                        read_outputs(s - 1, 1)
                    if u == HALF_END[0] + 1:
                        read_outputs(s, 0)

            step(0, 0)
            with act.Fori(0, (NQ - 2) // SLOTS) as i:
                for c in range(SLOTS):
                    step(i * SLOTS + (1 + c), 1)
            step(NQ - 1, NQ - 1)
            step(NQ, NQ)
            attn_round(0)
            attn_round(1)
            read_outputs(NQ - 1, 1)

            for t in range(1, NT - 1):
                attn_round(t + 1)
                if 0 <= t - LN_BEHIND < HT - 1:
                    ln_round(4, t - LN_BEHIND)
            ffn(1, 0)
            ffn(1, 1)

        @block.vector
        def _(dve):
            def ln_stat_of(l, t):
                b = l % 2
                if l < 2:
                    dve.wait_ge(x_loaded[b * HT + t], 16)
                else:
                    dve.wait_ge(x_added, (l // 2 - 1) * NT + b * HT + t + 1)
                dve.bn_stats(ln_stat[:, b, t, :], x_tok[:, b * HT + t, :]).then_inc(ln_stats, 1)
                dve.wait_ge(ln_stats, HT * l + t + 1)
                dve.bn_aggr(ln_mv[:, b, t, :], ln_stat[:, b, t, :]).then_inc(ln_mean, 1)

            def ln_norm(l, t):
                b = l % 2
                dve.wait_ge(ln_mean, HT * l + t + 1)
                dve.wait_ge(ln_rs, HT * l + t + 1)
                atleast(dve, ln_turned, HT * (l - 1) + t + 1)
                if l == 4:
                    dve.wait_ge(wout_lo_done, 1)
                dve.tensor_scalar(xn[:, t, :], x_tok[:, b * HT + t, :], ln_mv[:, b, t, 0:1],
                                  ln_rstd[:, b, t:t + 1], ALU.subtract, ALU.mult).then_inc(ln_normed, 1)

            def ln_rest(l, t):
                b, n = l % 2, HT * l + t
                cols = slice((b * HT + t) * P, (b * HT + t + 1) * P)
                dve.wait_ge(ln_hi, n + 1)
                dve.tensor_tensor(xnT_lo[:, :, cols], lnT_bank(l, t)[:, :].rearrange("p (a b) -> p a b", b=P),
                                  xnT_hi[:, :, cols].bitcast(F32), ALU.subtract).then_inc(ln_lo, 1)

            def each(f, l):
                for t in range(HT):
                    f(l, t)

            def lo_of(dst, src, hi):
                dve.tensor_tensor(dst, src, hi.bitcast(F32), ALU.subtract).then_inc(w_lo, 1)

            def ffn(n, b):
                r0, k0 = RAW_FFN[n] + b * FT, (2 * n + b) * FT

                def split_gate_up(k, parity):
                    slot, rs = (k0 + parity) % 2, (r0 + parity) % 2
                    wait_raw(dve, r0, k, parity)
                    dve.wait_ge(w_hi, k * 2 + (2 * r0 + 1))
                    atleast(dve, up_done, k + (k0 - 1))
                    lo_of(gu_lo[:, slot, :, :, :].rearrange("p a b c -> p (a b c)"), raw[:, rs, 0:2 * D],
                          gu_hi[:, slot, :, :, :].rearrange("p a b c -> p (a b c)"))

                def split_down(k, parity):
                    slot, rs = (k0 + parity) % 2, (r0 + parity) % 2
                    dve.wait_ge(w_hi, k * 2 + (2 * r0 + 2))
                    wait_down(dve, 2 * n + b, k)
                    lo_of(dn_lo[:, slot, :], raw[:, rs, 2 * D:], dn_hi[:, slot, :])

                def step(k, parity, more=True):
                    if more:
                        split_gate_up(k + 1, 1 - parity)
                    gated(k, parity)
                    if more:
                        split_down(k + 1, 1 - parity)

                def gated(k, parity):
                    slot = (k0 + parity) % 2
                    dve.wait_ge(silu_done, k + (k0 + 1))
                    dve.wait_ge(up_done, k + (k0 + 1))
                    atleast(dve, hid_lo_done, k + (k0 - 1))
                    atleast(dve, hid_hi_done, k + (k0 - 1))
                    dve.tensor_tensor(hid[:, slot, :], up_ps[slot][:, :], silu[:, slot, :],
                                      ALU.mult).then_inc(hid_done, 1)
                    dve.wait_ge(hid_hi_done, k + (k0 + 1))
                    dve.wait_ge(hid_done, k + (k0 + 1))
                    wait_down(dve, 2 * n + b, k)
                    dve.tensor_tensor(hid_lo[:, slot, :], hid[:, slot, :], hid_hi[:, slot, :].bitcast(F32),
                                      ALU.subtract).then_inc(hid_lo_done, 1)

                if b == 0:
                    split_gate_up(0, 0)
                    if n == 0:
                        each(ln_rest, 0)
                    else:
                        ln_rest(4, HT - 1)
                        add_attn(NT - 1)
                    split_down(0, 0)
                else:
                    add_y(n, 0)
                inside = LN_INSIDE.get((n, b))
                split_gate_up(1, 1)
                if inside:
                    each(ln_stat_of, inside)
                gated(0, 0)
                split_down(1, 1)
                if inside:
                    each(ln_norm, inside)
                    each(ln_rest, inside)
                step(1, 1)
                with dve.Fori(0, PAIRS) as i:
                    step(i * 2 + 2, 0)
                    step(i * 2 + 3, 1)
                    if (n, b) == (0, 1):
                        for c, (lo, hi, cols) in enumerate(((wqk_lo, wqk_hi, slice(0, 2 * D)),
                                                            (wv_lo, wv_hi, slice(2 * D, 3 * D)))):
                            dve.wait_ge(wqkv_hi_done, i * 2 + (c + 1))
                            dve.tensor_tensor(lo[:, bass.ds(i, 1), :], raw_qkv[:, bass.ds(i, 1), cols],
                                              hi[:, bass.ds(i, 1), :].bitcast(F32),
                                              ALU.subtract).then_inc(wqkv_lo_done, 1)
                step(FT - 1, 0, more=b == 0)

            def add_y(n, b):
                for t in range(HT):
                    dve.wait_ge(y_done, HT * (2 * n + b) + t + 1)
                    dve.scalar_tensor_tensor(out=x_tok[:, b * HT + t, :], in0=y_ps[t][:, :], scalar=0.5,
                                             in1=x_tok[:, b * HT + t, :], op0=ALU.mult,
                                             op1=ALU.add).then_inc(x_added, 1)

            each(ln_stat_of, 0)
            each(ln_norm, 0)
            ffn(0, 0)
            ffn(0, 1)
            add_y(0, 1)
            each(ln_stat_of, 3)
            each(ln_norm, 3)
            dve.wait_ge(v_ones, 1)

            def qk_clip(t):
                slot = t % 2
                for c in range(2):
                    dve.wait_ge(qk_done, 2 * t + c + 1)
                    atleast(dve, qk_turned, t - 1)
                    dve.tensor_scalar(qk[:, slot, c, :], qk_ps[slot][c][:, :], CLIP, -CLIP, ALU.min,
                                      ALU.max).then_inc(clipped, 1)
                for c in range(2):
                    dve.wait_ge(clipped, 2 * t + c + 1)
                    dve.bn_stats(qk_stat[:, slot, c, :], qk[:, slot, c, :]).then_inc(qk_stats, 1)
                for c in range(2):
                    dve.wait_ge(qk_stats, 2 * t + c + 1)
                    ins = dve.bn_aggr(qk_mv[:, slot, c, :], qk_stat[:, slot, c, :])
                ins.then_inc(qk_mean, 1)

            def qk_norm(t):
                slot = t % 2
                dve.wait_ge(qk_mean, t + 1)
                dve.wait_ge(qk_rs, t + 1)
                for c in range(2):
                    ins = dve.tensor_scalar(qk[:, slot, c, :], qk[:, slot, c, :], qk_mv[:, slot, c, 0:1],
                                            qk_rstd[:, slot, c:c + 1], ALU.subtract, ALU.mult)
                ins.then_inc(qk_normed, 1)

            def rest1(t):
                slot, pair, cols = t % 2, (t // 2) % 2, slice((t % 2) * P, (t % 2 + 1) * P)
                dve.wait_ge(part0_done, t + 1)
                atleast(dve, part2_done, t - 1)
                for c in range(2):
                    ins = dve.tensor_tensor(qkT_rest[:, slot, c, :, :], qkT[:, slot, c, :, :],
                                            parts[:, pair, :, c, 0, cols], ALU.subtract)
                ins.then_inc(rest1_done, 1)

            def rest2(t):
                slot, pair, cols = t % 2, (t // 2) % 2, slice((t % 2) * P, (t % 2 + 1) * P)
                dve.wait_ge(part1_done, t + 1)
                for c in range(2):
                    ins = dve.tensor_tensor(parts[:, pair, :, c, 2, cols], qkT_rest[:, slot, c, :, :],
                                            parts[:, pair, :, c, 1, cols], ALU.subtract)
                ins.then_inc(part2_done, 1)

            def v_clip(t):
                dve.wait_ge(v_done, t + 1)
                dve.tensor_scalar(v_aug[:, t, 0:H * VC].rearrange("p (h c) -> p h c", c=VC)[:, :, 0:HD],
                                  v_ps[t % V_LEAD][:, :].rearrange("p (h c) -> p h c", c=HD), CLIP, -CLIP, ALU.min,
                                  ALU.max).then_inc(v_clipped, 1)

            for t in range(NT):
                qk_clip(t)
                if t > 1:
                    rest1(t - 2)
                qk_norm(t)
                if t > 2:
                    rest2(t - 3)
                if t < HT // 2:
                    for c in range(2):
                        ln_rest(3, 2 * t + c)
            dve.wait_ge(const_in, 16 * len(constants))

            def ring_a_use(s, k, parity, use):
                kind, what = use
                ps, ago = bank_a(s, parity, k)
                dve.wait_ge(ring_a_done, use_base(s) + (k + 1))
                if kind == "max":
                    h, c = what
                    width, diag = MAX_CHUNKS[c][2:]
                    if diag is None:
                        dve.reduce_max(maxp[:, h, c:c + 1], ps[:, 0:width], AX_X).then_inc(ring_a_used, 1)
                    else:
                        if not isinstance(s, int):
                            dve.sem_inc(chunk_seen, 1)
                        dve.tensor_tensor_reduce(masked[:, (parity + k) % RING, 0:width], ps[:, 0:width],
                                                 masks[:, HALF - width:HALF], 1.0, MASKED, ALU.add, ALU.max,
                                                 maxp[:, h, c:c + 1]).then_inc(ring_a_used, 1)
                elif kind == "maxT":
                    atleast(dve, max_out, s * 16)
                    dve.tensor_copy(maxT[:, :], ps[0:PARTS * QH * NT, 0:P // 2].bitcast(BF16)).then_inc(ring_a_used, 1)
                else:
                    store_outputs(s - 1, what, ps)

            v_clip(0)
            rest1(NT - 2)
            rest2(NT - 3)
            v_clip(1)
            rest1(NT - 1)
            rest2(NT - 2)
            v_clip(2)
            rest2(NT - 1)
            for t in range(3, NT):
                for k in range(early_uses(t, 0)[0], early_uses(t, DT - 1)[1]):
                    ring_a_use(-1, k, 0, early[k])
                v_clip(t)

            def split_max(s):
                n0 = s * 5
                flat = maxv[:, :, :].rearrange("p h t -> p (h t)")

                def join():
                    dve.wait_ge(ring_a_used, use_base(s))
                    dve.tensor_tensor(maxv[:, :, HT:NT], maxp[:, :, HT:NC:2], maxp[:, :, HT + 1:NC:2],
                                      ALU.max).then_inc(max_step, 1)
                    dve.tensor_copy(maxv[:, :, 0:HT], maxp[:, :, 0:HT]).then_inc(max_step, 1)
                    dve.wait_ge(max_step, n0 + 2)

                def first():
                    dve.tensor_scalar(max_parts[:, 0, :], flat, -1.0, None, ALU.mult).then_inc(max_step, 1)

                def rest():
                    dve.wait_ge(max_step, n0 + 3)
                    dve.scalar_tensor_tensor(out=maxr[:, :], in0=flat, scalar=-1.0, in1=max_parts[:, 0, :],
                                             op0=ALU.mult, op1=ALU.subtract).then_inc(max_step, 1)

                def second():
                    dve.wait_ge(max_step, n0 + 4)
                    dve.tensor_copy(max_parts[:, 1, :], maxr[:, :]).then_inc(max_step, 1)

                def third():
                    dve.wait_ge(max_step, n0 + 5)
                    dve.tensor_tensor(max_parts[:, 2, :], maxr[:, :], max_parts[:, 1, :],
                                      ALU.subtract).then_inc(max_parts_done, 1)

                return [join, first, rest, second, third]

            def attn_rest(t):
                dve.wait_ge(aT_hi_done, t + 1)
                dve.tensor_tensor(aT_lo[:, t % 2, :, :], attnT_ps[t % 2][:, :].rearrange("p (a b) -> p a b", b=P),
                                  aT_hi[:, t % 2, :, :].bitcast(F32), ALU.subtract).then_inc(aT_lo_done, 1)

            def store_outputs(s, b, ps):
                o = ps[:, :].rearrange("p (t h c) -> p t h c", t=HT, c=VW)
                dve.reciprocal(rsum[:, b, :, :], o[:, :, :, HD]).then_inc(rsum_done, 1)
                dve.wait_ge(rsum_done, s * 2 + (b + 1))
                if isinstance(s, int):
                    dst = attn[:, b * HT:(b + 1) * HT, s * QH * HD:(s + 1) * QH * HD]
                else:
                    dst = attn[:, b * HT:(b + 1) * HT, bass.ds(s * (QH * HD), QH * HD)]
                dve.tensor_tensor(dst.rearrange("p t (h c) -> p t h c", c=HD), o[:, :, :, 0:HD],
                                  rsum[:, b, :, :].unsqueeze(3).to_broadcast([P, HT, QH, HD]),
                                  ALU.mult).then_inc(ring_a_used, 1)

            def step(s, parity, kind):
                k = 0
                small = split_max(s) if 0 <= kind < NQ else []
                if small:
                    small.pop(0)()
                for place in steps_of(kind):
                    for uses in place:
                        for use in uses:
                            if kind == NQ and use == ("out", 1):
                                attn_rest(0)
                                attn_rest(1)
                            while small:
                                small.pop(0)()
                                if use[0] == "max":
                                    break
                            if kind >= 0 or k >= EARLY:
                                ring_a_use(s, k, parity, use)
                            k += 1

            parity0 = (n_uses(-1) + n_uses(0)) % RING
            step(-1, 0, -1)
            step(0, n_uses(-1) % RING, 0)
            with dve.Fori(0, (NQ - 2) // SLOTS) as i:
                for c in range(SLOTS):
                    step(i * SLOTS + (1 + c), parity0, 1)
            step(NQ - 1, parity0, NQ - 1)
            step(NQ, use_base(NQ) % RING, NQ)

            def add_attn(t):
                dve.wait_ge(proj_done, t + 1)
                dve.tensor_tensor(x_tok[:, t, :], proj_ps[t % 2][:, :], x_tok[:, t, :], ALU.add).then_inc(x_added, 1)

            for t in range(NT - 1):
                if t > 0:
                    attn_rest(t + 1)
                add_attn(t)
                if t < HT:
                    ln_stat_of(4, t)
                if 0 < t <= HT:
                    ln_norm(4, t - 1)
                if 0 <= t - LN_BEHIND < HT - 1:
                    ln_rest(4, t - LN_BEHIND)
            ffn(1, 0)
            ffn(1, 1)
            add_y(1, 1)


def _bf16_bits(a):
    return (np.ascontiguousarray(a, np.float32).view(np.uint32) >> 16).astype(np.uint16)


def _bf16_parts(a):
    rest, found = np.asarray(a, np.float32), []
    for _ in range(PARTS):
        part = (rest.view(np.uint32) & np.uint32(0xFFFF0000)).view(np.float32)
        found.append(part)
        rest = rest - part
    return found


def _bias_rows():
    slope = (1.0 / np.power(2.0, np.arange(1, H + 1) * (8 / H))).astype(np.float32)
    pos = np.arange(S)
    low = pos % 8
    high = pos - low
    q = np.zeros((H, N_BIAS, S), np.float32)
    k = np.ones((H, N_BIAS + PARTS, S), np.float32)
    for p, s in enumerate(_bf16_parts(slope)):
        for n, where in enumerate((high, low)):
            row = 4 * p + 2 * n
            q[:, row, :], k[:, row, :] = s[:, None], where
            q[:, row + 1, :], k[:, row + 1, :] = where, -s[:, None]
    return [_bf16_bits(a.reshape(NQ, QH, a.shape[1], S).transpose(0, 2, 1, 3)) for a in (q, k)]


def _constants():
    eye = np.eye(P, dtype=np.float32)
    upper = np.triu(np.ones((P, P), np.float32), 1) * np.float32(MASKED)
    bias_q, bias_k = _bias_rows()
    return {"ident": eye, "ident_b": _bf16_bits(eye), "mask": _bf16_bits(upper.T),
            "masks": np.concatenate([np.zeros((P, HALF - P), np.float32), upper], axis=1),
            "bias_q": bias_q, "bias_k": bias_k}


def kernel(L0_attn_hidden_states, L0_attn_w_qkv, L0_attn_q_ln_w, L0_attn_q_ln_b, L0_attn_k_ln_w, L0_attn_k_ln_b,
           L0_attn_w_out, L0_ffn_W_gate, L0_ffn_W_up, L0_ffn_W_down):
    import concourse.bacc as _bacc
    from concourse.bass_utils import run_bass_kernel_spmd as _run

    f32 = lambda a: np.asarray(a)
    w_ffn = np.zeros((FT, P, FFN_RAW), np.float32)
    for n, w in enumerate((f32(L0_ffn_W_gate), f32(L0_ffn_W_up))):
        padded = np.zeros((FT * P, D), np.float32)
        padded[0:F] = w
        w_ffn[:, :, n * D:(n + 1) * D] = padded.reshape(FT, P, DT, P).transpose(0, 3, 2, 1).reshape(FT, P, D)
    padded = np.zeros((FT * P, D), np.float32)
    padded[0:F] = f32(L0_ffn_W_down).T
    w_ffn[:, :, 2 * D:] = padded.reshape(FT, P, D)
    by_feature = np.arange(D).reshape(DT, P // HD, HD).transpose(0, 2, 1).ravel()
    order = np.concatenate([by_feature, D + by_feature, 2 * D + np.arange(D)])
    w_qkv = np.ascontiguousarray(f32(L0_attn_w_qkv)[order].T.reshape(DT, P, 3 * D).transpose(1, 0, 2))
    w_out = f32(L0_attn_w_out).T.reshape(DT, P, D).transpose(1, 0, 2)
    column = lambda a, b: np.stack([f32(a)[by_feature].reshape(DT, P).T,
                                   f32(b)[by_feature].reshape(DT, P).T], axis=1)
    arrays = {
        "x": f32(L0_attn_hidden_states).reshape(S, D),
        "w_ffn": w_ffn,
        "w_qkv": w_qkv,
        "w_out": w_out,
        "ln_w": column(L0_attn_q_ln_w, L0_attn_k_ln_w),
        "ln_b": column(L0_attn_q_ln_b, L0_attn_k_ln_b),
        **_constants(),
    }
    nc = _bacc.Bacc("TRN2", target_bir_lowering=False, num_devices=1)
    args = []
    for name, a in arrays.items():
        arrays[name] = np.ascontiguousarray(a)
        ap = nc.dram_tensor(name, a.shape, mybir.dt.from_np(a.dtype), kind="ExternalInput").ap()
        args.append(ap.bitcast(BF16) if a.dtype == np.uint16 else ap)
    out = nc.dram_tensor("y", (S, D), F32, kind="ExternalOutput").ap()
    x, w_f, w_q, w_o, l_w, l_b, ident, ident_b, mask, masks, bias_q, bias_k = args
    macaron_block(nc, x, w_f, w_q, w_o, l_w, l_b, ident, ident_b, mask, masks, bias_q, bias_k, out)
    r = _run(nc, [arrays], core_ids=[0])
    return r.results[0]["y"].reshape(1, S, D)
```
